# Optimizing a Trainium2 kernel written in Bass

```python
import numpy as np
import jax
import jax.numpy as jnp

def _softmax(x, axis=-1):
    return jax.nn.softmax(x, axis=axis)

def _gelu(x):
    return jax.nn.gelu(x, approximate=True)

def _silu(x):
    return jax.nn.silu(x)

def _sigmoid(x):
    return jax.nn.sigmoid(x)

def _layernorm(x, axis=-1, eps=1e-05):
    m = jnp.mean(x, axis=axis, keepdims=True)
    v = jnp.var(x, axis=axis, keepdims=True)
    return (x - m) / jnp.sqrt(v + eps)

def _scatter_add(tgt, idx, src, axis=0):
    return tgt.at[idx].add(src)

def _segment_sum(src, seg, n):
    return jax.ops.segment_sum(src, seg, n)
kernel_name = 'mk_xattn_ffn_d1_seqx_r8_73df2c'

def setup_inputs(seed: int=0):
    np.random.seed(seed)
    _w = jnp.asarray

    def _rec_inputs():
        import jax
        import jax.numpy as jnp
        _rk = jax.random.key(seed)
        x = 7.22e-05 + 1 * jax.random.normal(jax.random.fold_in(_rk, 1), (16, 128, 256), jnp.float32)
        _lenS = 128 - jax.random.randint(jax.random.fold_in(_rk, 7), (16,), 0, max(1, 128 // 4) + 1, jnp.int32)
        _lenS2 = 128 - jax.random.randint(jax.random.fold_in(_rk, 8), (16,), 0, max(1, 128 // 4) + 1, jnp.int32)
        _ctx_2048P = jax.random.normal(jax.random.fold_in(_rk, 11), (16, 16, 256), jnp.float32)
        _ctx_2048c = jax.random.dirichlet(jax.random.fold_in(_rk, 511), 0.3 * jnp.ones((16,), jnp.float32), (16, 128))
        _ctx_2048t = jnp.einsum('bsk,bkd->bsd', _ctx_2048c, _ctx_2048P)
        _ctx_2048t = _ctx_2048t * jax.lax.rsqrt(jnp.mean(jnp.square(_ctx_2048t)) + 1e-12) * 0.953939
        ctx_2048 = 4.13588e-05 + 0.999923 * (_ctx_2048t + 0.3 * jax.random.normal(jax.random.fold_in(_rk, 611), (16, 128, 256), jnp.float32))
        return (x, ctx_2048)
    x, ctx_2048 = _rec_inputs()

    def _L0_xattn_setup():
        import jax, jax.numpy as jnp
        import numpy as np
        N_HEAD = 8
        key = jax.random.key(seed)
        k1, k2, k3 = jax.random.split(key, 3)
        b, d, m = (4, 128, 256)
        c, n = (128, 256)
        q = jax.random.normal(k1, (b, d, m), dtype=jnp.float32)
        k = jax.random.normal(k2, (d // d * b, d, n), dtype=jnp.float32).reshape(b, d, n)
        v = jax.random.normal(k3, (b, c, n), dtype=jnp.float32)
        return {'q': q, 'k': k, 'v': v}
    _L0_xattn_all = _L0_xattn_setup()
    _L0_xattn_in = {k: v for k, v in _L0_xattn_all.items() if k in ()}
    del _L0_xattn_all

    def _L0_ffn_setup():
        import jax, jax.numpy as jnp
        import numpy as np
        from jax import lax
        B, S, H = (2, 64, 256)
        I = 96
        E = 64
        K = 8
        key = jax.random.key(seed)
        k1, k2, k3, k4 = jax.random.split(key, 4)
        hidden_states = jax.random.normal(k1, (B, S, H), jnp.float32)
        gate_weight = jax.random.normal(k2, (E, H), jnp.float32) * 0.02
        gate_up_weights = jax.random.normal(k3, (E, H, 2 * I), jnp.float32) * 0.02
        down_weights = jax.random.normal(k4, (E, I, H), jnp.float32) * 0.02
        return {'hidden_states': hidden_states, 'gate_weight': gate_weight, 'gate_up_weights': gate_up_weights, 'down_weights': down_weights}
    _L0_ffn_all = _L0_ffn_setup()
    _L0_ffn_in = {k: v for k, v in _L0_ffn_all.items() if k in ('gate_weight', 'gate_up_weights', 'down_weights')}
    del _L0_ffn_all
    return {'x': x, 'ctx_2048': ctx_2048, 'L0_ffn_gate_weight': _L0_ffn_in['gate_weight'], 'L0_ffn_gate_up_weights': _L0_ffn_in['gate_up_weights'], 'L0_ffn_down_weights': _L0_ffn_in['down_weights']}

def reference(x, ctx_2048, L0_ffn_gate_weight, L0_ffn_gate_up_weights, L0_ffn_down_weights):
    import jax
    import jax.numpy as jnp

    def _L0_xattn_ref(q, k, v):
        import jax, jax.numpy as jnp
        import numpy as np
        N_HEAD = 8
        b, d, m = q.shape
        c = v.shape[1]
        h = N_HEAD
        qh = q.reshape(b * h, d // h, m)
        kh = k.reshape(b * h, d // h, -1)
        vh = v.reshape(b * h, c // h, -1)
        scale = 1.0 / jnp.sqrt(jnp.asarray(d // h, dtype=q.dtype))
        qk = jnp.einsum('bdm,bdn->bmn', qh, kh) * scale
        sm = jax.nn.softmax(qk, axis=-1)
        ret = jnp.einsum('bmn,bcn->bcm', sm, vh)
        return ret.reshape(b, c, m)

    def _L0_ffn_ref(hidden_states, gate_weight, gate_up_weights, down_weights):
        import jax, jax.numpy as jnp
        import numpy as np
        from jax import lax
        B, S, H = (2, 64, 256)
        I = 96
        E = 64
        K = 8
        orig_shape = hidden_states.shape
        x = hidden_states.reshape(-1, H)
        T = x.shape[0]
        logits = x @ gate_weight.T
        probs = jax.nn.softmax(logits.astype(jnp.float32), axis=-1)
        routing_weights, selected_experts = lax.top_k(probs, K)
        wsum = routing_weights.sum(axis=-1, keepdims=True)
        wsum = jnp.where(wsum == 0, 1.0, wsum)
        routing_weights = (routing_weights / wsum).astype(x.dtype)
        combine = jnp.zeros((T, E), x.dtype).at[jnp.arange(T)[:, None], selected_experts].add(routing_weights)

        def body(acc, ws):
            wgu, wd, we = ws
            gu = x @ wgu
            gate, up = jnp.split(gu, 2, axis=-1)
            act = jax.nn.silu(gate) * up
            out = act @ wd
            return (acc + we[:, None] * out, None)
        init = jnp.zeros_like(x)
        final, _ = lax.scan(body, init, (gate_up_weights, down_weights, combine.T))
        return final.reshape(orig_shape)
    x = x + _L0_xattn_ref(_layernorm(x, axis=-1), ctx_2048, ctx_2048)
    x = x + _L0_ffn_ref(_layernorm(x, axis=-1), L0_ffn_gate_weight, L0_ffn_gate_up_weights, L0_ffn_down_weights)
    return x

_drawn_inputs = setup_inputs


def setup_inputs(seed=0):
    import zlib

    import numpy as np

    out = dict(_drawn_inputs(seed))
    spreads = {}
    factors = {'L0_ffn_gate_weight': 8.0, 'L0_ffn_gate_up_weights': 8.0, 'L0_ffn_down_weights': 8.0}
    for name, (base, spread) in spreads.items():
        noise = np.random.default_rng([zlib.crc32(name.encode()), seed]).standard_normal(out[name].shape)
        drawn = base * np.exp(spread * noise) if base else spread * noise
        out[name] = jnp.asarray(drawn.astype(out[name].dtype))
    for name, factor in factors.items():
        out[name] = (out[name] * factor).astype(out[name].dtype)
    return out
```

```python
from contextlib import ExitStack

import concourse.bass as bass
from concourse import mybir

F32 = mybir.dt.float32
BF16 = mybir.dt.bfloat16
ALU = mybir.AluOpType
ACT = mybir.ActivationFunctionType
AX = mybir.AxisListType

P = 128
EPS = 1e-5
LOWEST = -3.0e38
PARTS = 3
PRODUCTS = 6
RING = 4


def build(nc, x, ctx_in, gate_w, gate_up_w, down_w, out):
    NB, ROWS, M = x.shape
    H = 8
    D = ROWS // H
    MT = M // P
    NE = gate_w.shape[0]
    I2 = gate_up_w.shape[2]
    I = I2 // 2
    K8 = 8
    TOK = NB * ROWS
    CH = 512
    NCH = TOK // CH
    QSCALE = float(D) ** -0.5
    STACK = PRODUCTS * D
    NPAIR = H // 2
    V = D + 1
    PEELED = RING + 1
    NG = NB // 2
    STEP_AHEAD = 3

    with ExitStack() as es:
        def sb(name, shape, dt=F32):
            return es.enter_context(nc.sbuf_tensor(name, shape, dt))

        def ps(name, shape, dt=F32):
            return es.enter_context(nc.psum_tensor(name, shape, dt))

        def sem(name):
            return es.enter_context(nc.semaphore(name))

        X = sb("X", [P, NB, M])
        CT = sb("CT", [P, RING, M])
        yT = sb("yT", [P, MT, TOK])
        q_ln = sb("q_ln", [P, 2, M])
        q_res = sb("q_res", [P, M])
        k_res = sb("k_res", [P, M])
        q_parts = sb("q_parts", [P, 2, PARTS, 2, M], BF16)
        k_parts = sb("k_parts", [P, 2, PARTS, 2, M], BF16)
        q_stack = sb("q_stack", [P, RING, H, M], BF16)
        k_stack = sb("k_stack", [P, RING, H, M], BF16)
        vT = sb("vT", [P, 2, MT, H, V])
        pT = sb("pT", [P, NPAIR, 2, MT, M])
        negmax = sb("negmax", [P, 2, H, MT])
        nm_res = sb("nm_res", [P, H, MT])
        nm_parts = sb("nm_parts", [P, 2, MT, PARTS, H], BF16)
        nm_rows = sb("nm_rows", [STACK, 2, M], BF16)
        pick = sb("pick", [STACK, H, P], BF16)
        rsum = sb("rsum", [P, MT, H])
        o_norm = sb("o_norm", [P, MT, P])
        stats1 = sb("stats1", [P, 6])
        mv1 = sb("mv1", [P, 2, 2])
        rstd1 = sb("rstd1", [P, 2])
        stats2 = sb("stats2", [P, 6])
        mv2 = sb("mv2", [P, 2])
        rstd2 = sb("rstd2", [P, 2])
        y = sb("y", [P, M])
        y_now = sb("y_now", [P, MT, P])
        minus_half = sb("minus_half", [P, 1])
        ident = sb("ident", [P, P])
        ident16 = sb("ident16", [P, P], BF16)
        gw = sb("gw", [NE, M])
        gwT = sb("gwT", [P, MT, NE])
        logits = sb("logits", [P, NB, NE])
        lg_now = sb("lg_now", [P, NE])
        top_now = sb("top_now", [P, K8])
        rest_now = sb("rest_now", [P, NE])
        weights = sb("weights", [P, NB, NE])
        wsum = sb("wsum", [P, NB])
        winv = sb("winv", [P, NB])
        wgu = sb("wgu", [P, 2, MT, I2])
        wd = sb("wd", [I, 2, M])
        silu = sb("silu", [I, 2, CH])
        hT = sb("hT", [I, 2, CH])

        q_dram = nc.dram_tensor("q_parts_dram", [NG, PARTS, 2 * H, D, M], BF16).ap()
        k_dram = nc.dram_tensor("k_parts_dram", [NG, PARTS, 2 * H, D, M], BF16).ap()

        s_ps = ps("s_ps", [P, 2, MT, M])
        st_ps = ps("st_ps", [P, 2, 2, MT, M])
        o_ps = ps("o_ps", [P, 512])
        m_ps = ps("m_ps", [P, 512])
        O = o_ps[:, 0:MT * H * V].rearrange("p (t h v) -> p t h v", t=MT, h=H)
        M0 = m_ps[:, 0:M]
        M1 = m_ps[:, M:2 * M]
        LG = M1[:, 0:NE]
        st_flat = [st_ps[:, k].rearrange("p i t m -> p i (t m)") for k in range(2)]
        down_ps = [s_ps[:, k, 0, :] for k in range(2)]
        NM16 = M1[:, P:2 * P].bitcast(BF16)

        x_in = [sem("x_first"), sem("x_rest")]
        c_in = [sem("c_in0"), sem("c_in1")]
        gw_in = sem("gw_in")
        consts = sem("consts")
        vt_ones = sem("vt_ones")
        gw_t = sem("gw_t")
        gw_ready = sem("gw_ready")
        ln1_stats = sem("ln1_stats")
        ln1_aggr = sem("ln1_aggr")
        ln1_var = sem("ln1_var")
        ln1_rstd = sem("ln1_rstd")
        q_ready = sem("q_ready")
        split_hi = sem("split_hi")
        split_res = sem("split_res")
        split_mid = sem("split_mid")
        q_split = sem("q_split")
        parts_ready = sem("parts_ready")
        parts_stored = sem("parts_stored")
        stacks_in = [sem("stacks_in0"), sem("stacks_in1")]
        s_ready = sem("s_ready")
        max_done = sem("max_done")
        nm_hi = sem("nm_hi")
        nm_r = sem("nm_r")
        nm_mid = sem("nm_mid")
        nm_split = sem("nm_split")
        nm_t = sem("nm_t")
        nm_ready = sem("nm_ready")
        v_t = sem("v_t")
        v_ready = sem("v_ready")
        st_ready = sem("st_ready")
        exp_done = sem("exp_done")
        pv_done = sem("pv_done")
        rs_done = sem("rs_done")
        norm_done = sem("norm_done")
        o_t = sem("o_t")
        x1_done = sem("x1_done")
        ln2_stats = sem("ln2_stats")
        ln2_aggr = sem("ln2_aggr")
        ln2_var = sem("ln2_var")
        ln2_rstd = sem("ln2_rstd")
        y_ready = sem("y_ready")
        y_t = sem("y_t")
        yt_ready = sem("yt_ready")
        yt_kept = sem("yt_kept")
        lg_ready = sem("lg_ready")
        lg_read = sem("lg_read")
        top_done = sem("top_done")
        rest_done = sem("rest_done")
        shift_done = sem("shift_done")
        chosen_done = sem("chosen_done")
        route = sem("route")
        e_ready = sem("e_ready")
        wd_in = [sem("w_in0"), sem("w_in1")]
        gu_ready = sem("gu_ready")
        silu_done = sem("silu_done")
        h_ready = sem("h_ready")
        down_ready = sem("down_ready")
        acc_done = sem("acc_done")
        store = sem("store")

        block = es.enter_context(nc.Block())

        xv = x.rearrange("b p m -> p b m")
        cv = ctx_in.rearrange("b p m -> p b m")

        def wait_alone(eng, semaphore, value):
            eng.wait_ge(semaphore, value)
            if not isinstance(value, int):
                eng.nop(nofuse=True)

        def steps(eng, body):
            for b in range(PEELED):
                body(b, b)
            with eng.Fori(0, (NB - PEELED - STEP_AHEAD) // RING) as i:
                for j in range(PEELED, PEELED + RING):
                    body(i * RING + j, j)
            for b in range(NB - STEP_AHEAD, NB):
                body(b, b)

        @block.sync
        def _(sp):
            def load_ctx(g, gp, first):
                if not first:
                    sp.wait_ge(v_t, g * 2 - 2)
                    wait_alone(sp, parts_ready, g * 2 - 2)
                sp.dma_start(CT[:, 2 * gp:2 * gp + 2, :], cv[:, bass.ds(g * 2, 2), :]).then_inc(c_in[gp], 16)

            load_ctx(0, 0, True)
            sp.dma_start(X[:, 0:2, :], xv[:, 0:2, :]).then_inc(x_in[0], 16)
            sp.dma_start(gw[:, :], gate_w).then_inc(gw_in, 16)
            load_ctx(1, 1, True)
            sp.dma_start(X[:, 2:NB, :], xv[:, 2:NB, :]).then_inc(x_in[1], 16)

            def stack_group(g, gp, first):
                wait_alone(sp, parts_ready, g * 2 + 2)
                for parts, dram in ((q_parts, q_dram), (k_parts, k_dram)):
                    sp.dma_start(dram[bass.ds(g, 1)].rearrange("a t (b h) d m -> (h d) (a t b) m", b=2),
                                 parts[:, gp].rearrange("p t b m -> p (t b) m")).then_inc(parts_stored, 16)
                wait_alone(sp, parts_stored, g * 32 + 32)
                if not first:
                    wait_alone(sp, st_ready, (g * 2 - 2) * NPAIR)
                row = 0
                for k_of_q, (a, n) in enumerate(((0, 3), (1, 2), (2, 1))):
                    for r in range(n):
                        for stack, dram, part in ((q_stack, q_dram, a), (k_stack, k_dram, r)):
                            src = dram[bass.ds(g, 1), part].rearrange("a bh d m -> d (a bh) m")
                            sp.dma_start(
                                stack[row:row + D, 2 * gp:2 * gp + 2].rearrange("p b h m -> p (b h) m"),
                                src).then_inc(stacks_in[gp], 16)
                        row += D

            stack_group(0, 0, True)
            stack_group(1, 1, True)
            with sp.Fori(1, NG // 2) as i:
                for gp in range(2):
                    load_ctx(i * 2 + gp, gp, False)
                    stack_group(i * 2 + gp, gp, False)

            def load_expert(e, w, first):
                if not first:
                    wait_alone(sp, down_ready, (e - 1) * NB)
                sp.dma_start(wgu[:, w], gate_up_w[bass.ds(e, 1)].rearrange("a (t p) n -> p (a t) n", p=P)
                             ).then_inc(wd_in[w], 16)
                sp.dma_start(wd[:, w, :], down_w[bass.ds(e, 1)].rearrange("a i m -> i (a m)")
                             ).then_inc(wd_in[w], 16)

            load_expert(0, 0, True)
            load_expert(1, 1, True)
            with sp.Fori(1, NE // 2) as i:
                for w in range(2):
                    load_expert(i * 2 + w, w, False)
            sp.wait_ge(acc_done, NE * NB)
            sp.dma_start(out.rearrange("b p m -> p b m"), X[:, :, :]).then_inc(store, 16)
            sp.wait_ge(store, 16)

        @block.gpsimd
        def _(pool):
            pool.memset(ident[:], 0.0).then_inc(consts, 1)
            pool.memset(ident16[:], 0.0).then_inc(consts, 1)
            pool.memset(pick[:], 0.0).then_inc(consts, 1)
            pool.memset(nm_rows[:], 0.0).then_inc(consts, 1)
            pool.memset(minus_half[:], -0.5).then_inc(consts, 1)
            pool.memset(vT[:], 1.0).then_inc(vt_ones, 1)
            pool.wait_ge(consts, 5)
            for m in (ident, ident16):
                pool.affine_select(out=m[:], in_=m[:], compare_op=ALU.not_equal, fill=1.0, base=0,
                                   pattern=[[-1, P]], channel_multiplier=1).then_inc(consts, 1)
            for t in range(PARTS):
                pool.wait_ge(consts, 5 + 2 + t)
                pool.affine_select(out=pick[:], in_=pick[:], compare_op=ALU.not_equal, fill=1.0,
                                   base=-t * H, pattern=[[-1, H], [0, P]],
                                   channel_multiplier=1).then_inc(consts, 1)

            def split(b, j):
                gp, bb = (j // 2) % 2, j % 2
                pool.wait_ge(c_in[gp], (b + (RING - j % RING)) * 4)
                if not (isinstance(b, int) and b < RING):
                    pool.wait_ge(parts_stored, (b - bb) * 16 - 32)
                wait_alone(pool, q_ready, b + 1)
                for n, (src, res, parts) in enumerate(((q_ln[:, bb, :], q_res, q_parts),
                                                       (CT[:, j % RING, :], k_res, k_parts))):
                    hi, mid, lo = (parts[:, gp, t, bb, :] for t in range(PARTS))
                    pool.tensor_copy(hi, src).then_inc(split_hi, 1)
                    pool.wait_ge(split_hi, b * 2 + n + 1)
                    pool.tensor_tensor(res[:], src, hi, ALU.subtract).then_inc(split_res, 1)
                    wait_alone(pool, split_res, b * 2 + n + 1)
                    pool.tensor_copy(mid, res[:]).then_inc(split_mid, 1)
                    pool.wait_ge(split_mid, b * 2 + n + 1)
                    last = pool.tensor_tensor(lo, res[:], mid, ALU.subtract)
                    if n == 1:
                        last.then_inc(parts_ready, 1)
                    else:
                        last.then_inc(q_split, 1)

            def rstd(sem_in, sem_var, sem_out, b, mv, out_):
                wait_alone(pool, sem_in, b + 1)
                pool.tensor_scalar(out_[:, 0:1], mv[:, 1:2], EPS, None, ALU.add).then_inc(sem_var, 1)
                pool.wait_ge(sem_var, b + 1)
                pool.tensor_tensor(out_[:, 1:2], out_[:, 0:1], minus_half[:], ALU.pow).then_inc(sem_out, 1)

            def split_max(b, j):
                par = j % 2
                pool.wait_ge(max_done, (b + 1) * H)
                if not (isinstance(b, int) and b < 2):
                    wait_alone(pool, nm_t, b - 1)
                src = negmax[:, par]
                hi, mid, lo = (nm_parts[:, par, :, t, :].rearrange("p t h -> p h t") for t in range(PARTS))
                pool.tensor_copy(hi, src).then_inc(nm_hi, 1)
                pool.wait_ge(nm_hi, b + 1)
                pool.tensor_tensor(nm_res[:], src, hi, ALU.subtract).then_inc(nm_r, 1)
                wait_alone(pool, nm_r, b + 1)
                pool.tensor_copy(mid, nm_res[:]).then_inc(nm_mid, 1)
                pool.wait_ge(nm_mid, b + 1)
                pool.tensor_tensor(lo, nm_res[:], mid, ALU.subtract).then_inc(nm_split, 1)

            def keep_yT(b):
                wait_alone(pool, yt_ready, b + 1)
                pool.tensor_copy(yT[:, :, bass.ds(b * P, P)], y_now[:]).then_inc(yt_kept, 1)

            for b in range(STEP_AHEAD):
                rstd(ln1_aggr, ln1_var, ln1_rstd, b, mv1[:, b % 2], rstd1)
                split(b, b)
            split_max(0, 0)

            def step(b, j):
                first, last = j == 0, isinstance(b, int) and b == NB - 1
                if not (isinstance(b, int) and b + STEP_AHEAD >= NB):
                    rstd(ln1_aggr, ln1_var, ln1_rstd, b + STEP_AHEAD, mv1[:, (j + STEP_AHEAD) % 2], rstd1)
                if not first:
                    rstd(ln2_aggr, ln2_var, ln2_rstd, b - 1, mv2, rstd2)
                if not last:
                    split_max(b + 1, j + 1)
                if not (isinstance(b, int) and b + STEP_AHEAD >= NB):
                    split(b + STEP_AHEAD, j + STEP_AHEAD)
                if not first:
                    keep_yT(b - 1)

            steps(pool, step)
            rstd(ln2_aggr, ln2_var, ln2_rstd, NB - 1, mv2, rstd2)
            keep_yT(NB - 1)

        @block.vector
        def _(dve):
            def ln1(b, j):
                bb = j % 2
                if isinstance(b, int):
                    dve.wait_ge(x_in[0 if b < 2 else 1], 16)
                xb = X[:, bass.ds(b, 1), :].rearrange("p a m -> p (a m)")
                dve.bn_stats(stats1[:], xb).then_inc(ln1_stats, 1)
                wait_alone(dve, ln1_stats, b + 1)
                dve.bn_aggr(mv1[:, bb, :], stats1[:]).then_inc(ln1_aggr, 1)

            def ln1_apply(b, j):
                bb = j % 2
                dve.wait_ge(ln1_rstd, b + 1)
                if not (isinstance(b, int) and b < 2):
                    dve.wait_ge(q_split, b - 1)
                xb = X[:, bass.ds(b, 1), :].rearrange("p a m -> p (a m)")
                dve.tensor_scalar(q_ln[:, bb, :], xb, mv1[:, bb, 0:1], rstd1[:, 1:2],
                                  ALU.subtract, ALU.mult).then_inc(q_ready, 1)

            def head_max(b, j, h):
                dve.wait_ge(s_ready, b * H + (h + 1))
                if h == 0 and not (isinstance(b, int) and b < 2):
                    dve.wait_ge(nm_split, b - 1)
                dve.tensor_reduce(negmax[:, j % 2, h, :], s_ps[:, h % 2], AX.X, ALU.max,
                                  negate=True).then_inc(max_done, 1)

            def normalise(b):
                dve.wait_ge(pv_done, b * NPAIR + NPAIR)
                dve.reciprocal(rsum[:].rearrange("p t (h o) -> p t h o", o=1), O[:, :, :, D:V]).then_inc(rs_done, 1)
                dve.wait_ge(rs_done, b + 1)
                if not (isinstance(b, int) and b < 1):
                    dve.wait_ge(o_t, b)
                dve.tensor_tensor(o_norm[:].rearrange("p t (h d) -> p t h d", h=H), O[:, :, :, 0:D],
                                  rsum[:].rearrange("p t (h o) -> p t h o", o=1).to_broadcast([P, MT, H, D]),
                                  ALU.mult).then_inc(norm_done, 1)

            def residual(b):
                xb = X[:, bass.ds(b, 1), :].rearrange("p a m -> p (a m)")
                dve.wait_ge(o_t, b + 1)
                dve.tensor_tensor(xb, xb, M1, ALU.add).then_inc(x1_done, 1)
                wait_alone(dve, x1_done, b + 1)
                dve.bn_stats(stats2[:], xb).then_inc(ln2_stats, 1)
                wait_alone(dve, ln2_stats, b + 1)
                dve.bn_aggr(mv2[:], stats2[:]).then_inc(ln2_aggr, 1)

            def ln2_apply(b):
                xb = X[:, bass.ds(b, 1), :].rearrange("p a m -> p (a m)")
                dve.wait_ge(ln2_rstd, b + 1)
                if not (isinstance(b, int) and b < 1):
                    dve.wait_ge(y_t, b)
                dve.tensor_scalar(y[:], xb, mv2[:, 0:1], rstd2[:, 1:2],
                                  ALU.subtract, ALU.mult).then_inc(y_ready, 1)

            def top8(b):
                lg = logits[:, bass.ds(b, 1), :].rearrange("p a e -> p (a e)")
                ch = weights[:, bass.ds(b, 1), :].rearrange("p a e -> p (a e)")
                dve.wait_ge(lg_ready, b + 1)
                dve.tensor_copy(lg_now[:], LG).then_inc(lg_read, 1)
                wait_alone(dve, lg_read, b + 1)
                dve.max(top_now[:], lg_now[:]).then_inc(top_done, 1)
                wait_alone(dve, top_done, b + 1)
                dve.match_replace(rest_now[:], top_now[:], lg_now[:], LOWEST).then_inc(rest_done, 1)
                dve.tensor_scalar(lg, lg_now[:], top_now[:, 0:1], None, ALU.subtract).then_inc(shift_done, 1)
                dve.wait_ge(rest_done, b + 1)
                dve.tensor_tensor(ch, rest_now[:], lg_now[:], ALU.not_equal).then_inc(chosen_done, 1)
                dve.wait_ge(shift_done, b + 1)
                dve.wait_ge(chosen_done, b + 1)

            for b in range(STEP_AHEAD):
                ln1(b, b)
                ln1_apply(b, b)
            for h in range(H):
                head_max(0, 0, h)

            def step(b, j):
                first, last = j == 0, isinstance(b, int) and b == NB - 1
                ahead = not (isinstance(b, int) and b + STEP_AHEAD >= NB)
                if ahead:
                    ln1(b + STEP_AHEAD, j + STEP_AHEAD)
                if not last:
                    head_max(b + 1, j + 1, 0)
                    head_max(b + 1, j + 1, 1)
                if not first:
                    normalise(b - 1)
                if ahead:
                    ln1_apply(b + STEP_AHEAD, j + STEP_AHEAD)
                if not last:
                    head_max(b + 1, j + 1, 2)
                    head_max(b + 1, j + 1, 3)
                if not first:
                    residual(b - 1)
                if not last:
                    head_max(b + 1, j + 1, 4)
                    head_max(b + 1, j + 1, 5)
                if not first:
                    ln2_apply(b - 1)
                if not last:
                    head_max(b + 1, j + 1, 6)
                    head_max(b + 1, j + 1, 7)
                if not first:
                    top8(b - 1)

            steps(dve, step)
            normalise(NB - 1)
            residual(NB - 1)
            ln2_apply(NB - 1)
            top8(NB - 1)

            n = [0]

            def link(ins):
                n[0] += 1
                ins.then_inc(route, 1)
                dve.wait_ge(route, n[0])

            def wide(t):
                return t.rearrange("p (b o) -> p b o", o=1).to_broadcast([P, NB, NE])

            dve.wait_ge(e_ready, 1)
            link(dve.tensor_tensor(weights[:], weights[:], logits[:], ALU.mult))
            link(dve.tensor_reduce(wsum[:], weights[:], AX.X, ALU.add))
            link(dve.tensor_single_scalar(winv[:], wsum[:], 0.0, ALU.is_equal))
            link(dve.tensor_tensor(wsum[:], wsum[:], winv[:], ALU.add))
            link(dve.reciprocal(winv[:], wsum[:]))
            link(dve.tensor_tensor(weights[:], weights[:], wide(winv[:]), ALU.mult))

            def up_times_silu(e, c):
                n = c % 2
                dve.wait_ge(silu_done, e * NCH + (c + 1))
                dve.tensor_tensor(hT[:, n, :], silu[:, n, :], st_flat[1][0:I, n, :], ALU.mult
                                  ).then_inc(h_ready, 1)

            def accumulate(e, w, t):
                dve.wait_ge(down_ready, e * NB + (t + 1))
                if True:
                    if not (isinstance(e, int) and e == 0):
                        dve.wait_ge(acc_done, e * NB + (t + 1) - NB)
                dve.scalar_tensor_tensor(X[:, t, :], down_ps[t % 2], weights[:, t, bass.ds(e, 1)], X[:, t, :],
                                         op0=ALU.mult, op1=ALU.add).then_inc(acc_done, 1)

            def expert(e, w):
                up_times_silu(e, 0)
                for c in range(1, NCH):
                    up_times_silu(e, c)
                    for t in range((c - 1) * CH // P, c * CH // P):
                        accumulate(e, w, t)
                for t in range((NCH - 1) * CH // P, NB):
                    accumulate(e, w, t)

            expert(0, 0)
            with dve.Fori(1, NE) as e:
                expert(e, 0)

        @block.scalar
        def _(act):
            act.wait_ge(gw_t, 1)
            act.copy(gwT[:].rearrange("p t e -> p (t e)"), M0[:, 0:MT * NE]).then_inc(gw_ready, 1)

            def copy_v(b, j):
                act.wait_ge(v_t, b + 1)
                if isinstance(b, int) and b == 0:
                    act.wait_ge(vt_ones, 1)
                if not (isinstance(b, int) and b < 2):
                    act.wait_ge(pv_done, b * NPAIR - NPAIR)
                act.copy(vT[:, j % 2, :, :, 0:D], M0.rearrange("p (t h d) -> p t h d", t=MT, h=H)
                         ).then_inc(v_ready, 1)

            def copy_negmax(b, j):
                act.wait_ge(nm_t, b + 1)
                if not (isinstance(b, int) and b < 2):
                    act.wait_ge(st_ready, b * NPAIR - NPAIR)
                act.copy(nm_rows[0:PARTS * H, j % 2, :], NM16[0:PARTS * H, :]).then_inc(nm_ready, 1)

            def exps(b, pair):
                act.wait_ge(st_ready, b * NPAIR + (pair + 1))
                if not (isinstance(b, int) and b == 0):
                    act.wait_ge(pv_done, b * NPAIR + (pair + 1 - NPAIR))
                act.activation(pT[:, pair], st_ps[:, pair % 2], ACT.Exp, scale=QSCALE).then_inc(exp_done, 1)

            def copy_yT(b):
                act.wait_ge(y_t, b + 1)
                if not (isinstance(b, int) and b < 1):
                    act.wait_ge(lg_ready, b)
                    act.wait_ge(yt_kept, b)
                act.copy(y_now[:], M0.rearrange("p (t n) -> p t n", t=MT)).then_inc(yt_ready, 1)

            copy_v(0, 0)
            copy_negmax(0, 0)

            def step(b, j):
                first, last = j == 0, isinstance(b, int) and b == NB - 1
                exps(b, 0)
                if not last:
                    copy_v(b + 1, j + 1)
                exps(b, 1)
                exps(b, 2)
                if not first:
                    copy_yT(b - 1)
                exps(b, 3)
                if not last:
                    copy_negmax(b + 1, j + 1)

            steps(act, step)
            copy_yT(NB - 1)
            act.wait_ge(shift_done, NB)
            act.activation(logits[:], logits[:], ACT.Exp).then_inc(e_ready, 1)

            def expert(e):
                for c in range(NCH):
                    n = c % 2
                    act.wait_ge(gu_ready, e * NCH + (c + 1))
                    if not (isinstance(e, int) and e == 0 and c < 2):
                        act.wait_ge(h_ready, e * NCH + (c - 1))
                    act.activation(silu[:, n, :], st_flat[0][0:I, n, :], ACT.Silu).then_inc(silu_done, 1)

            expert(0)
            with act.Fori(1, NE) as e:
                expert(e)

        @block.tensor
        def _(pe):
            pe.wait_ge(consts, 5 + 2 + PARTS)
            pe.wait_ge(gw_in, 16)
            for t in range(MT):
                last = pe.transpose(M0[:, t * NE:(t + 1) * NE], gw[:, t * P:(t + 1) * P], ident[0:NE, 0:NE])
            last.then_inc(gw_t, 1)

            def transpose_v(b, j):
                pe.wait_ge(c_in[(j // 2) % 2], (b + (RING - j % RING)) * 4)
                if isinstance(b, int) and b == 0:
                    pe.wait_ge(gw_ready, 1)
                else:
                    pe.wait_ge(nm_ready, b)
                if not (isinstance(b, int) and b < 3):
                    pe.wait_ge(lg_read, b - 2)
                for t in range(MT):
                    last = pe.transpose(M0[:, t * P:(t + 1) * P],
                                        CT[:, j % RING, t * P:(t + 1) * P], ident[:])
                last.then_inc(v_t, 1)

            def scores(b, j, h):
                if h == 0:
                    pe.wait_ge(stacks_in[(j // 2) % 2],
                               (b + (RING - j % RING)) * (2 * PRODUCTS * 16 // RING))
                if not (isinstance(b, int) and b == 0 and h < 2):
                    pe.wait_ge(max_done, b * H + (h - 1))
                r = j % RING
                for t in range(MT):
                    last = pe.matmul(s_ps[:, h % 2, t, :], q_stack[0:STACK, r, h, t * P:(t + 1) * P],
                                     k_stack[0:STACK, r, h, :], start=True, stop=True)
                last.then_inc(s_ready, 1)

            def scores_t(b, j, pair):
                if pair == 0:
                    pe.wait_ge(nm_ready, b + 1)
                if not (isinstance(b, int) and b == 0 and pair < 2):
                    pe.wait_ge(exp_done, b * NPAIR + (pair - 1))
                r = j % RING
                for i in range(2):
                    h = 2 * pair + i
                    for t in range(MT):
                        pe.matmul(st_ps[:, pair % 2, i, t, :], k_stack[0:STACK, r, h, t * P:(t + 1) * P],
                                  q_stack[0:STACK, r, h, :], start=True, stop=False)
                        last = pe.matmul(st_ps[:, pair % 2, i, t, :], pick[:, h, :],
                                         nm_rows[:, j % 2, :], start=False, stop=True)
                last.then_inc(st_ready, 1)

            def values(b, j, pair):
                pe.wait_ge(exp_done, b * NPAIR + (pair + 1))
                if pair == 0:
                    pe.wait_ge(v_ready, b + 1)
                    if not (isinstance(b, int) and b == 0):
                        pe.wait_ge(norm_done, b)
                for i in range(2):
                    h = 2 * pair + i
                    for t in range(MT):
                        for k in range(MT):
                            last = pe.matmul(O[:, t, h, :], pT[:, pair, i, k, t * P:(t + 1) * P],
                                             vT[:, j % 2, k, h, :], start=(k == 0), stop=(k == MT - 1))
                last.then_inc(pv_done, 1)

            def transpose_o(b, j):
                pe.wait_ge(norm_done, b + 1)
                pe.wait_ge(v_ready, b + 3)
                for t in range(MT):
                    last = pe.transpose(M1[:, t * P:(t + 1) * P], o_norm[:, t, :], ident[:])
                last.then_inc(o_t, 1)

            def transpose_y(b, j):
                pe.wait_ge(y_ready, b + 1)
                for t in range(MT):
                    last = pe.transpose(M0[:, t * P:(t + 1) * P], y[:, t * P:(t + 1) * P], ident[:])
                last.then_inc(y_t, 1)

            def gate(b, last):
                pe.wait_ge(yt_ready, b + 1)
                if not last:
                    pe.wait_ge(nm_ready, b + 3)
                for t in range(MT):
                    last = pe.matmul(LG, y_now[:, t, :], gwT[:, t, :], start=(t == 0), stop=(t == MT - 1))
                last.then_inc(lg_ready, 1)

            def transpose_negmax(b, j):
                pe.wait_ge(nm_split, b + 1)
                pe.wait_ge(v_ready, b + 1)
                if not (isinstance(b, int) and b < 2):
                    pe.wait_ge(yt_ready, b - 1)
                for t in range(MT):
                    last = pe.transpose(NM16[0:PARTS * H, t * P:(t + 1) * P],
                                        nm_parts[:, j % 2, t].rearrange("p t h -> p (t h)"), ident16[:])
                last.then_inc(nm_t, 1)

            transpose_v(0, 0)
            for h in range(H):
                scores(0, 0, h)
            transpose_negmax(0, 0)

            def step(b, j):
                first, last = j == 0, isinstance(b, int) and b == NB - 1
                if not first:
                    values(b - 1, j - 1, 3)
                if not last:
                    scores(b + 1, j + 1, 0)
                    scores(b + 1, j + 1, 1)
                scores_t(b, j, 0)
                if not last:
                    transpose_v(b + 1, j + 1)
                    scores(b + 1, j + 1, 2)
                scores_t(b, j, 1)
                if not last:
                    scores(b + 1, j + 1, 3)
                    scores(b + 1, j + 1, 4)
                if not first:
                    transpose_o(b - 1, j - 1) if not last else transpose_o_last(b - 1, j - 1)
                values(b, j, 0)
                if not last:
                    scores(b + 1, j + 1, 5)
                scores_t(b, j, 2)
                if not last:
                    scores(b + 1, j + 1, 6)
                    scores(b + 1, j + 1, 7)
                values(b, j, 1)
                if not first:
                    pe.wait_ge(x1_done, b)
                    transpose_y(b - 1, j - 1)
                scores_t(b, j, 3)
                if not last:
                    transpose_negmax(b + 1, j + 1)
                values(b, j, 2)
                if not first:
                    gate(b - 1, last)

            def transpose_o_last(b, j):
                pe.wait_ge(norm_done, b + 1)
                pe.wait_ge(lg_read, b)
                for t in range(MT):
                    last = pe.transpose(M1[:, t * P:(t + 1) * P], o_norm[:, t, :], ident[:])
                last.then_inc(o_t, 1)

            steps(pe, step)
            values(NB - 1, NB - 1, 3)
            transpose_o_last(NB - 1, NB - 1)
            pe.wait_ge(x1_done, NB)
            transpose_y(NB - 1, NB - 1)
            gate(NB - 1, True)

            def gate_up(e, w, c):
                n = c % 2
                if c == 0:
                    pe.wait_ge(wd_in[w], (e + (2 - w)) * 16)
                if not (isinstance(e, int) and e == 0 and c < 2):
                    pe.wait_ge(h_ready, e * NCH + (c - 1))
                for half in range(2):
                    for t in range(MT):
                        last = pe.matmul(st_flat[half][0:I, n, :], wgu[:, w, t, half * I:(half + 1) * I],
                                         yT[:, t, c * CH:(c + 1) * CH], start=(t == 0), stop=(t == MT - 1))
                last.then_inc(gu_ready, 1)

            def down(e, w, c):
                n = c % 2
                pe.wait_ge(h_ready, e * NCH + (c + 1))
                for i in range(CH // P):
                    t = c * CH // P + i
                    if not (isinstance(e, int) and e == 0 and t < 2):
                        pe.wait_ge(acc_done, e * NB + (t - 1))
                    pe.matmul(down_ps[t % 2], hT[:, n, i * P:(i + 1) * P], wd[:, w, :],
                              start=True, stop=True).then_inc(down_ready, 1)

            def expert(e, w):
                gate_up(e, w, 0)
                for c in range(1, NCH):
                    gate_up(e, w, c)
                    down(e, w, c - 1)
                down(e, w, NCH - 1)

            pe.wait_ge(yt_kept, NB)
            expert(0, 0)
            expert(1, 1)
            with pe.Fori(1, NE // 2) as i:
                for w in range(2):
                    expert(i * 2 + w, w)


_INS = ['x', 'ctx_2048', 'L0_ffn_gate_weight', 'L0_ffn_gate_up_weights', 'L0_ffn_down_weights']


def kernel(**inputs):
    import numpy as _np
    import concourse.bacc as _bacc
    from concourse import mybir as _mybir
    from concourse.bass_utils import run_bass_kernel_spmd as _run

    nc = _bacc.Bacc("TRN2", target_bir_lowering=False, num_devices=1)
    arrays, args = {}, []
    for name in _INS:
        a = _np.ascontiguousarray(inputs[name])
        arrays[f"in_{name}"] = a
        args.append(nc.dram_tensor(f"in_{name}", a.shape, _mybir.dt.from_np(a.dtype), kind="ExternalInput").ap())
    args.append(nc.dram_tensor("out_dram", inputs["x"].shape, F32, kind="ExternalOutput").ap())
    build(nc, *args)
    r = _run(nc, [arrays], core_ids=[0])
    return r.results[0]["out_dram"]
```

```python
from contextlib import ExitStack

import concourse.bass as bass
from concourse import mybir

F32 = mybir.dt.float32
BF16 = mybir.dt.bfloat16
I32 = mybir.dt.int32
ALU = mybir.AluOpType
ACT = mybir.ActivationFunctionType
AX = mybir.AxisListType

P = 128
EPS = 1e-5
LOWEST = -3.0e38
PARTS = 3
PRODUCTS = 6
RING = 4
CAP = 352


def tiles_of(n):
    return [(a, min(P, n - a)) for a in range(0, n, P)]


def build(nc, x, ctx_in, gate_w, gate_up_w, down_w, out):
    NB, ROWS, M = x.shape
    H = 8
    D = ROWS // H
    MT = M // P
    NE = gate_w.shape[0]
    I2 = gate_up_w.shape[2]
    I = I2 // 2
    K8 = 8
    TOK = NB * ROWS
    QSCALE = float(D) ** -0.5
    STACK = PRODUCTS * D
    NPAIR = H // 2
    NG = NB // 2
    AHEAD = 4
    Y_LAG = 2
    LAG = 3
    SEND_LAG = 4
    QUAD = 32
    CT = tiles_of(CAP)
    NC = len(CT)
    SLOTS = CAP + 2
    ROW = M + NE + 1
    XROWS = NE * SLOTS
    CH = 512
    NCH = TOK // CH


    def live(n, count):
        return not isinstance(n, int) or 0 <= n < count

    def late(n, first):
        return not isinstance(n, int) or n >= first

    with ExitStack() as es:
        def sb(name, shape, dt=F32):
            return es.enter_context(nc.sbuf_tensor(name, shape, dt))

        def ps(name, shape, dt=F32):
            return es.enter_context(nc.psum_tensor(name, shape, dt))

        def sem(name):
            return es.enter_context(nc.semaphore(name))

        def sems(name, n):
            return [sem(f"{name}{i}") for i in range(n)]

        X = sb("X", [P, NB, M])
        qk = sb("qk", [P, RING, 2, M])
        qk_res = sb("qk_res", [P, 2, M])
        parts = sb("parts", [P, 2, 2, PARTS, 2, M], BF16)
        q_stack = sb("q_stack", [P, 2, H, 2, M], BF16)
        k_stack = sb("k_stack", [P, 2, H, 2, M], BF16)
        vT = sb("vT", [P, RING, MT, NPAIR, 2, QUAD])
        ones = sb("ones", [P, 2, QUAD])
        pT = sb("pT", [P, 2, NPAIR, 2, MT, M])
        negmax = sb("negmax", [P, 2, H, MT])
        nm_res = sb("nm_res", [P, H, MT])
        nm_parts = sb("nm_parts", [P, 2, MT, PARTS, H], BF16)
        nm_rows = sb("nm_rows", [STACK, 2, M], BF16)
        pick = sb("pick", [STACK, H, P], BF16)
        att = sb("att", [P, M])
        share = sb("share", [P, M])
        stats1 = sb("stats1", [P, 6])
        mv1 = sb("mv1", [P, 2, 2])
        rstd1 = sb("rstd1", [P, 2, 2])
        stats2 = sb("stats2", [P, 6])
        mv2 = sb("mv2", [P, 2])
        rstd2 = sb("rstd2", [P, 2])
        minus_half = sb("minus_half", [P, 1])
        ident = sb("ident", [P, P])
        ident16 = sb("ident16", [P, P], BF16)
        gw = sb("gw", [NE, M])
        gwT = sb("gwT", [P, MT, NE])
        y_now = sb("y_now", [P, MT, P])
        row = sb("row", [P, RING, ROW])
        yT_all = sb("yT_all", [P, MT, TOK])
        w_all = sb("w_all", [P, NB, NE])
        lg_now = sb("lg_now", [P, NE])
        top_now = sb("top_now", [P, K8])
        neg_top = sb("neg_top", [P, 1])
        rest_now = sb("rest_now", [P, NE])
        e_now = sb("e_now", [P, NE])
        chosen = sb("chosen", [P, 2, NE], BF16)
        before = sb("before", [P, 2, NE], BF16)
        lower = sb("lower", [P, P], BF16)
        ones16 = sb("ones16", [P, P], BF16)
        first_slot = sb("first_slot", [P, NE])
        slot_now = sb("slot_now", [P, NE])
        picked = sb("picked", [P, NE])
        slot_masked_t = sb("slot_masked_t", [P, NE])
        wsum = sb("wsum", [P, 4])
        top_slot = sb("top_slot", [P, K8])
        slots = sb("slots", [P, RING, K8], I32)
        number = sb("number", [P, NE], I32)
        token_i = sb("token_i", [P, NB], I32)
        token = sb("token", [P, NB])
        trash = sb("trash", [P, NC])
        count = sb("count", [P, NE])
        few = sb("few", [P, NE])
        most = sb("most", [P, 1])
        start = sb("start", [P, NC, NE])
        start_f = sb("start_f", [P, NE])
        start_i = sb("start_i", [P, NC - 1, NE], I32)
        new = sb("new", [P, NE])
        is_new = sb("is_new", [P, NE, NC])
        past = sb("past", [P, NE, NC])
        most_i = sb("most_i", [P, 1], I32)
        wgu = sb("wgu", [P, RING, MT, I2])
        wd = sb("wd", [I, RING, M])
        rows = sb("rows", [P, RING, NC, ROW])
        yT = sb("yT", [P, 2, MT, CAP])
        silu = sb("silu", [I, 2, CAP])
        hT = sb("hT", [I, 2, CAP])
        w3 = sb("w3", [P, RING, NC])
        num_new = sb("num_new", [P, NC])
        to = sb("to", [P, RING, NC], I32)
        ys = sb("ys", [P, RING, NC, M])

        parts_dram = nc.dram_tensor("parts_dram", [NG, 2, PARTS, H, D, 2, M], BF16).ap()
        xg = nc.dram_tensor("rows_by_expert", [XROWS, ROW], F32).ap()
        acc = [nc.dram_tensor(f"acc{i}", [TOK + P, M], F32).ap() for i in range(NC)]

        s_ps = ps("s_ps", [P, 2, MT, M])
        st_ps = ps("st_ps", [P, 2, 2, MT, M])
        o_ps = ps("o_ps", [P, 2, M])
        m_ps = ps("m_ps", [P, 2 * M])
        M0 = m_ps[:, 0:M]
        LG = m_ps[:, 0:NE]
        NM16 = m_ps[:, 0:P].bitcast(BF16)
        t_ps = [st_ps[:, 0, t].rearrange("p t m -> p (t m)") for t in range(MT)]
        g_ps = [s_ps[:, n].rearrange("p t m -> p (t m)") for n in range(2)]
        u_ps = [st_ps[:, 1, n].rearrange("p t m -> p (t m)") for n in range(2)]
        d_ps = [o_ps[:, 0, :], o_ps[:, 1, :], m_ps[:, 0:M]]

        pT_flat = pT[:].rearrange("p a b c d m -> p (a b c d m)")
        silu_d = pT_flat[0:I, 0:2 * CH].rearrange("p (n c) -> p n c", n=2)
        hT_d = pT_flat[0:I, 2 * CH:4 * CH].rearrange("p (n c) -> p n c", n=2)
        gd_ps = [st_ps[:, 0, n].rearrange("p t m -> p (t m)") for n in range(2)]
        ud_ps = [st_ps[:, 1, n].rearrange("p t m -> p (t m)") for n in range(2)]
        dd_ps = [s_ps[:, 0, 0, :], s_ps[:, 1, 0, :], o_ps[:, 0, :], M0]
        DOWN = len(dd_ps)
        FB = 4
        fin = pT_flat[:, 0:2 * NC * FB * M].rearrange("p (n c b m) -> p n c b m", n=2, c=NC, b=FB)
        RK = m_ps[:, 0:NE]
        ACC_CLEARS = (NC - 1) * len(range(0, (TOK + P) * M // P, RING * NC * M)) + 1
        zeros = ys[:].rearrange("p r c m -> p (r c m)")
        ZW = RING * NC * M
        assert (TOK + P) * M // P <= 2 * ZW

        before_done = sem("before_done")
        gw_in = sem("gw_in")
        consts = sem("consts")
        zeroed = sem("zeroed")
        rows_clear = sem("rows_clear")
        tables = sem("tables")
        gw_t = sem("gw_t")
        gw_ready = sem("gw_ready")
        ln1_stats = sem("ln1_stats")
        ln1_aggr = sem("ln1_aggr")
        ln1_var = sem("ln1_var")
        ln1_rstd = sem("ln1_rstd")
        q_ready = sem("q_ready")
        split_hi = sem("split_hi")
        split_res = sem("split_res")
        split_mid = sem("split_mid")
        parts_ready = sem("parts_ready")
        s_ready = sem("s_ready")
        max_done = sem("max_done")
        nm_hi = sem("nm_hi")
        nm_r = sem("nm_r")
        nm_mid = sem("nm_mid")
        nm_split = sem("nm_split")
        nm_t = sem("nm_t")
        nm_ready = sem("nm_ready")
        v_t = sem("v_t")
        v_ready = sem("v_ready")
        st_ready = sem("st_ready")
        exp_done = sem("exp_done")
        pv_done = sem("pv_done")
        recip_done = sem("recip_done")
        att_done = sem("att_done")
        x1_done = sem("x1_done")
        ln2_stats = sem("ln2_stats")
        ln2_aggr = sem("ln2_aggr")
        ln2_var = sem("ln2_var")
        ln2_rstd = sem("ln2_rstd")
        y_ready = sem("y_ready")
        y_t = sem("y_t")
        yt_ready = sem("yt_ready")
        yt_kept = sem("yt_kept")
        row_number = sem("row_number")
        w_kept = sem("w_kept")
        lg_ready = sem("lg_ready")
        lg_read = sem("lg_read")
        top_done = sem("top_done")
        neg_done = sem("neg_done")
        rest_done = sem("rest_done")
        chosen_done = sem("chosen_done")
        e_ready = sem("e_ready")
        picked_done = sem("picked_done")
        wsum_done = sem("wsum_done")
        guard_done = sem("guard_done")
        wsum1_done = sem("wsum1_done")
        winv_done = sem("winv_done")
        row_w = sem("row_w")
        rank_ready = sem("rank_ready")
        slot_wide = sem("slot_wide")
        slot_masked = sem("slot_masked")
        slot_top = sem("slot_top")
        slots_ready = sem("slots_ready")
        acc_clear = sem("acc_clear")
        x1_kept = sem("x1_kept")
        count_ready = sem("count_ready")
        plan_done = sem("plan_done")
        flag_ready = sem("flag_ready")
        t_ready = sem("t_ready")
        yt0 = sem("yt0")
        yt1 = sem("yt1")
        gu_ready = sem("gu_ready")
        silu_done = sem("silu_done")
        h_ready = sem("h_ready")
        down_ready = sem("down_ready")
        ys01 = sem("ys01")
        ys2 = sem("ys2")
        w_ready = sem("w_ready")
        pad_ready = sem("pad_ready")
        to_ready = sem("to_ready")
        gu_ready_d = sem("gu_ready_d")
        silu_done_d = sem("silu_done_d")
        h_ready_d = sem("h_ready_d")
        down_ready_d = sem("down_ready_d")
        acc_done_d = sem("acc_done_d")
        fin_add = sem("fin_add")
        fin_ready = sem("fin_ready")
        out_in = sem("out_in")
        x_in = sems("x_in", 2)
        c_in = sems("c_in", 2)
        parts_stored = sems("parts_stored", 2)
        stacks_in = sems("stacks_in", 2)
        row_sent = sems("row_sent", RING)
        rows_in = sems("rows_in", RING)
        weights_in = sems("weights_in", RING)
        added = sems("added", NC)
        fin_in = sems("fin_in", 2)
        fin_out = sems("fin_out", 2)
        dense_in = sems("dense_in", 2)

        block = es.enter_context(nc.Block())

        xv = x.rearrange("b p m -> p b m")
        cv = ctx_in.rearrange("b p m -> p b m")
        ov = out.rearrange("b p m -> p b m")

        def wait_alone(eng, semaphore, value):
            eng.wait_ge(semaphore, value)
            if not isinstance(value, int):
                eng.nop(nofuse=True)

        def ring_steps(eng, body, count, tail):
            for b in range(RING):
                body(b, b)
            with eng.Fori(1, count // RING - 1) as i:
                for j in range(RING):
                    body(i * RING + j, j)
            for b in range(count - RING, count + tail):
                body(b, b)

        def steps(eng, body):
            ring_steps(eng, body, NB, LAG)

        def expert_steps(eng, body, tail):
            ring_steps(eng, body, NE, tail)

        def rounds(n, j, each):
            return (n + (RING - j % RING)) * (each // RING)

        @block.sync
        def _(sp):
            def store_chunk(sp, k):
                sp.wait_ge(fin_ready, k + 1)
                sp.dma_start(ov[:, k * FB:(k + 1) * FB, :], fin[:, k % 2, 0]).then_inc(fin_out[k % 2], 16)

            def load_ctx(g, gp):
                if late(g, 2):
                    sp.wait_ge(v_t, g * 2 - 2)
                    wait_alone(sp, split_res, g * 2 - 2)
                sp.dma_start(qk[:, 2 * gp:2 * gp + 2, 1, :], cv[:, bass.ds(g * 2, 2), :]).then_inc(c_in[gp], 16)

            def stack_group(g, gp):
                wait_alone(sp, parts_ready, g * 2 + 2)
                sp.dma_start(parts_dram[bass.ds(g, 1)].rearrange("a k t h d b m -> (h d) (a k t) (b m)"),
                             parts[:, gp].rearrange("p k t b m -> p (k t) (b m)")).then_inc(parts_stored[gp], 16)
                wait_alone(sp, parts_stored[gp], (g + (2 - gp)) * 8)
                if late(g, 2):
                    wait_alone(sp, st_ready, (g * 2 - 2) * NPAIR)
                row0 = 0
                for a in range(PARTS):
                    n = PARTS - a
                    for t in range(n):
                        src = parts_dram[bass.ds(g, 1), 1, t].rearrange("a h d b m -> d (a h) (b m)")
                        sp.dma_start(k_stack[row0 + t * D:row0 + (t + 1) * D, gp].rearrange("p h b m -> p h (b m)"),
                                     src).then_inc(stacks_in[gp], 16)
                    for t in range(n):
                        src = parts_dram[bass.ds(g, 1), 0, a].rearrange("a h d b m -> d (a h) (b m)")
                        sp.dma_start(q_stack[row0:row0 + D, gp].rearrange("p h b m -> p h (b m)"),
                                     src).then_inc(stacks_in[gp], 16)
                        row0 += D

            load_ctx(0, 0)
            sp.dma_start(X[:, 0:2, :], xv[:, 0:2, :]).then_inc(x_in[0], 16)
            sp.dma_start(gw[:, :], gate_w).then_inc(gw_in, 16)
            load_ctx(1, 1)
            sp.dma_start(X[:, 2:NB, :], xv[:, 2:NB, :]).then_inc(x_in[1], 16)
            stack_group(0, 0)
            stack_group(1, 1)
            load_ctx(2, 0)
            stack_group(2, 0)
            load_ctx(3, 1)
            stack_group(3, 1)
            sp.wait_ge(zeroed, 1)
            for c in range(1, NC):
                flat = acc[c].rearrange("n m -> (n m)").rearrange("(p f) -> p f", p=P)
                for a in range(0, (TOK + P) * M // P, ZW):
                    w = min(ZW, (TOK + P) * M // P - a)
                    sp.dma_start(flat[:, a:a + w], zeros[:, 0:w]).then_inc(acc_clear, 16)
            sp.dma_start(acc[0][TOK:TOK + P, :], zeros[:, 0:M]).then_inc(acc_clear, 16)
            with sp.Fori(2, NG // 2) as i:
                for gp in range(2):
                    load_ctx(i * 2 + gp, gp)
                    stack_group(i * 2 + gp, gp)
            sp.wait_ge(x1_done, NB)
            sp.dma_start(acc[0][0:TOK, :].rearrange("(b p) m -> p b m", p=P), X[:, :, :]).then_inc(x1_kept, 16)

            def load_rows(e, j):
                r = j % RING
                if late(e, RING):
                    wait_alone(sp, t_ready, e - (RING - 1))
                    wait_alone(sp, to_ready, e - (RING - 1))
                for c, (a, n) in enumerate(CT):
                    if c == 0:
                        first = e * SLOTS
                    else:
                        first = sp.value_load(start_i[0:1, c - 1, bass.ds(e, 1)], min_val=0, max_val=XROWS - P)
                    sp.dma_start(rows[0:n, r, c, :], xg[bass.ds(first, n), :]).then_inc(rows_in[r], 16)

            def load_weights(e, j):
                r = j % RING
                if late(e, RING):
                    wait_alone(sp, down_ready, e * NC - (RING - 1) * NC)
                sp.dma_start(wgu[:, r], gate_up_w[bass.ds(e, 1)].rearrange("a (t p) n -> p (a t) n", p=P)
                             ).then_inc(weights_in[r], 16)
                sp.dma_start(wd[:, r, :], down_w[bass.ds(e, 1)].rearrange("a i m -> i (a m)")
                             ).then_inc(weights_in[r], 16)

            def load_step(e, j):
                if live(e + 1, NE):
                    load_rows(e + 1, j + 1)
                if late(e, RING):
                    load_weights(e, j)

            for e in range(RING):
                load_weights(e, e)
            sp.wait_ge(flag_ready, 1)
            busiest = sp.value_load(most_i[0:1, 0:1], min_val=0, max_val=TOK)
            with sp.If(busiest < CAP + 1):
                for n in range(RING):
                    sp.wait_ge(row_sent[n], NB // RING * K8 * 16)
                sp.wait_ge(rows_clear, 1)
                load_rows(0, 0)
                expert_steps(sp, load_step, 0)

                for c in range(NC):
                    sp.wait_ge(added[c], NE * 16)
                for k in range(NB // FB):
                    n = k % 2
                    if k >= 2:
                        sp.wait_ge(fin_out[n], 16 * (k // 2))
                    for c in range(NC):
                        sp.dma_start(fin[:, n, c],
                                     acc[c][k * FB * P:(k + 1) * FB * P, :].rearrange("(b p) m -> p b m", p=P)
                                     ).then_inc(fin_in[n], 16)
                    if k >= 1:
                        store_chunk(sp, k - 1)
                store_chunk(sp, NB // FB - 1)
                for n in range(2):
                    sp.wait_ge(fin_out[n], 16 * (NB // FB // 2))
            with sp.Else():
                def load_dense(e, w):
                    if late(e, 2):
                        wait_alone(sp, down_ready_d, (e - 1) * NB)
                    sp.dma_start(wgu[:, w], gate_up_w[bass.ds(e, 1)].rearrange("a (t p) n -> p (a t) n", p=P)
                                 ).then_inc(dense_in[w], 16)
                    sp.dma_start(wd[:, w, :], down_w[bass.ds(e, 1)].rearrange("a i m -> i (a m)")
                                 ).then_inc(dense_in[w], 16)

                for n in range(RING):
                    sp.wait_ge(weights_in[n], 32)
                load_dense(0, 0)
                load_dense(1, 1)
                with sp.Fori(1, NE // 2) as i:
                    for w in range(2):
                        load_dense(i * 2 + w, w)
                sp.wait_ge(acc_done_d, NE * NB)
                sp.dma_start(ov, X[:, :, :]).then_inc(out_in, 16)
                sp.wait_ge(out_in, 16)
            sp.wait_ge(x1_kept, 16)
            sp.wait_ge(acc_clear, 16 * ACC_CLEARS)
            for n in range(RING):
                sp.wait_ge(row_sent[n], NB // RING * K8 * 16)

        @block.gpsimd
        def _(pool):
            pool.memset(ident[:], 0.0).then_inc(consts, 1)
            pool.memset(ident16[:], 0.0).then_inc(consts, 1)
            pool.memset(minus_half[:], -0.5).then_inc(consts, 1)
            pool.wait_ge(consts, 3)
            for m in (ident, ident16):
                pool.affine_select(out=m[:], in_=m[:], compare_op=ALU.not_equal, fill=1.0, base=0,
                                   pattern=[[-1, P]], channel_multiplier=1).then_inc(consts, 1)

            def rstd(sem_in, sem_var, sem_out, b, mv, out_):
                wait_alone(pool, sem_in, b + 1)
                pool.tensor_scalar(out_[:, 0:1], mv[:, 1:2], EPS, None, ALU.add).then_inc(sem_var, 1)
                pool.wait_ge(sem_var, b + 1)
                pool.tensor_tensor(out_[:, 1:2], out_[:, 0:1], minus_half[:], ALU.pow).then_inc(sem_out, 1)

            def rstd_1(b, j):
                rstd(ln1_aggr, ln1_var, ln1_rstd, b, mv1[:, j % 2], rstd1[:, j % 2])

            for b in range(2):
                rstd_1(b, b)
            pool.memset(pick[:], 0.0).then_inc(consts, 1)
            pool.memset(nm_rows[:], 0.0).then_inc(consts, 1)
            for t in range(PARTS):
                pool.wait_ge(consts, 7 + t)
                pool.affine_select(out=pick[:], in_=pick[:], compare_op=ALU.not_equal, fill=1.0,
                                   base=-t * H, pattern=[[-1, H], [0, P]],
                                   channel_multiplier=1).then_inc(consts, 1)
            for b in range(2, AHEAD):
                rstd_1(b, b)
            pool.memset(vT[:], 0.0).then_inc(consts, 1)
            pool.memset(ones[:], 0.0).then_inc(consts, 1)
            pool.wait_ge(consts, 12)
            for i in range(2):
                pool.memset(ones[:, i, i * D:(i + 1) * D], 1.0).then_inc(consts, 1)
            pool.memset(ones16[:], 1.0).then_inc(tables, 1)
            pool.memset(before[:], 0.0).then_inc(tables, 1)
            pool.iota(token_i[:], pattern=[[P, NB]], base=1, channel_multiplier=1).then_inc(tables, 1)
            pool.iota(number[:], pattern=[[SLOTS, NE]], base=1, channel_multiplier=0).then_inc(tables, 1)
            pool.wait_ge(tables, 4)
            pool.affine_select(out=lower[:], in_=ones16[:], compare_op=ALU.is_gt, fill=0.0, base=0,
                               pattern=[[1, P]], channel_multiplier=-1).then_inc(tables, 1)
            pool.tensor_copy(token[:], token_i[:]).then_inc(tables, 1)
            pool.tensor_copy(first_slot[:], number[:]).then_inc(tables, 1)
            pool.wait_ge(tables, 7)
            pool.iota(number[:, 0:NC], pattern=[[0, NC]], base=TOK + 1, channel_multiplier=1).then_inc(tables, 1)
            pool.wait_ge(tables, 8)
            pool.tensor_copy(trash[:], number[:, 0:NC]).then_inc(tables, 1)
            pool.memset(rows[:], 0.0).then_inc(rows_clear, 1)

            def send(b, j, half):
                pool.wait_ge(row_number, b + 1)
                pool.wait_ge(w_kept, b + 1)
                pool.wait_ge(row_w, b + 1)
                wait_alone(pool, slots_ready, b + 1)
                for k in range(half * K8 // 2, (half + 1) * K8 // 2):
                    pool.indirect_dma_start(xg, bass.IndirectOffsetOnAxis(ap=slots[:, j % RING, k:k + 1], axis=0),
                                            row[:, j % RING, :], None).then_inc(row_sent[j % RING], 16)

            def step(b, j):
                if live(b - SEND_LAG, NB):
                    send(b - SEND_LAG, j - SEND_LAG, 0)
                if live(b - Y_LAG, NB):
                    rstd(ln2_aggr, ln2_var, ln2_rstd, b - Y_LAG, mv2, rstd2)
                if live(b + AHEAD, NB):
                    rstd_1(b + AHEAD, j + AHEAD)
                if live(b - SEND_LAG, NB):
                    send(b - SEND_LAG, j - SEND_LAG, 1)

            ring_steps(pool, step, NB, SEND_LAG)

            def add_rows(e, j):
                r = j % RING
                wait_alone(pool, to_ready, e + 1)
                for c, (a, n) in enumerate(CT):
                    if late(e, 1):
                        wait_alone(pool, added[c], e * 16)
                    if c == 0:
                        wait_alone(pool, ys01, e + 1)
                    if c == NC - 1:
                        wait_alone(pool, ys2, e + 1)
                    pool.indirect_dma_start(acc[c], bass.IndirectOffsetOnAxis(ap=to[0:n, r, c:c + 1], axis=0),
                                            ys[0:n, r, c, :], None, compute_op=ALU.add).then_inc(added[c], 16)

            pool.wait_ge(flag_ready, 1)
            busiest = pool.value_load(most_i[0:1, 0:1], min_val=0, max_val=TOK)
            with pool.If(busiest < CAP + 1):
                pool.wait_ge(acc_clear, ACC_CLEARS * 16)
                pool.wait_ge(x1_kept, 16)
                expert_steps(pool, lambda e, j: add_rows(e, j) if live(e, NE) else None, 0)

        @block.vector
        def _(dve):
            def batch(t, b):
                return t[:, bass.ds(b, 1), :].rearrange("p a m -> p (a m)")

            def ln1(b, j):
                if isinstance(b, int):
                    dve.wait_ge(x_in[0 if b < 2 else 1], 16)
                if late(b, 1):
                    wait_alone(dve, ln1_aggr, b)
                dve.bn_stats(stats1[:], batch(X, b)).then_inc(ln1_stats, 1)
                if late(b, 2):
                    dve.wait_ge(q_ready, b - 1)
                wait_alone(dve, ln1_stats, b + 1)
                dve.bn_aggr(mv1[:, j % 2, :], stats1[:]).then_inc(ln1_aggr, 1)

            def ln1_apply(b, j):
                dve.wait_ge(ln1_rstd, b + 1)
                if late(b, RING):
                    dve.wait_ge(split_res, b - (RING - 1))
                dve.tensor_scalar(qk[:, j % RING, 0, :], batch(X, b), mv1[:, j % 2, 0:1], rstd1[:, j % 2, 1:2],
                                  ALU.subtract, ALU.mult).then_inc(q_ready, 1)

            def part_of(j, t):
                return parts[:, (j // 2) % 2, :, t, j % 2, :]

            def residual(b, j):
                if late(b, 1):
                    dve.wait_ge(parts_ready, b)
                dve.wait_ge(split_hi, b + 1)
                dve.tensor_tensor(qk_res[:], qk[:, j % RING], part_of(j, 0), ALU.subtract).then_inc(split_res, 1)

            def third_part(b, j):
                dve.wait_ge(split_mid, b + 1)
                dve.tensor_tensor(part_of(j, 2), qk_res[:], part_of(j, 1), ALU.subtract).then_inc(parts_ready, 1)

            def head_max(b, j, h):
                if h == 0 and late(b, 2):
                    dve.wait_ge(nm_split, b - 1)
                dve.wait_ge(s_ready, b * H + (h + 1))
                dve.tensor_reduce(negmax[:, j % 2, h, :], s_ps[:, h % 2], AX.X, ALU.max,
                                  negate=True).then_inc(max_done, 1)

            def split_max(b, j):
                par = j % 2
                dve.wait_ge(max_done, (b + 1) * H)
                if late(b, 2):
                    dve.wait_ge(nm_t, b - 1)
                if late(b, 1):
                    dve.wait_ge(nm_split, b)
                src = negmax[:, par]
                hi, mid, lo = (nm_parts[:, par, :, t, :].rearrange("p t h -> p h t") for t in range(PARTS))
                dve.tensor_copy(hi, src).then_inc(nm_hi, 1)
                dve.wait_ge(nm_hi, b + 1)
                dve.tensor_tensor(nm_res[:], src, hi, ALU.subtract).then_inc(nm_r, 1)
                dve.wait_ge(nm_r, b + 1)
                dve.tensor_copy(mid, nm_res[:]).then_inc(nm_mid, 1)
                dve.wait_ge(nm_mid, b + 1)
                dve.tensor_tensor(lo, nm_res[:], mid, ALU.subtract).then_inc(nm_split, 1)

            def attend(b):
                dve.wait_ge(pv_done, b + 1)
                if late(b, 1):
                    dve.wait_ge(x1_done, b)
                dve.reciprocal(share[:], o_ps[:, 1, :]).then_inc(recip_done, 1)
                dve.wait_ge(recip_done, b + 1)
                dve.tensor_tensor(att[:], o_ps[:, 0, :], share[:], ALU.mult).then_inc(att_done, 1)
                dve.wait_ge(att_done, b + 1)
                dve.tensor_tensor(batch(X, b), batch(X, b), att[:], ALU.add).then_inc(x1_done, 1)

            def ln2(b):
                if late(b, 1):
                    dve.wait_ge(y_ready, b)
                wait_alone(dve, x1_done, b + 1)
                dve.bn_stats(stats2[:], batch(X, b)).then_inc(ln2_stats, 1)
                wait_alone(dve, ln2_stats, b + 1)
                dve.bn_aggr(mv2[:], stats2[:]).then_inc(ln2_aggr, 1)

            def ln2_apply(b, j):
                dve.wait_ge(ln2_rstd, b + 1)
                if late(b, RING):
                    dve.wait_ge(row_sent[j % RING], (b - j % RING) * (K8 * 16 // RING))
                dve.tensor_scalar(row[:, j % RING, 0:M], batch(X, b), mv2[:, 0:1], rstd2[:, 1:2],
                                  ALU.subtract, ALU.mult).then_inc(y_ready, 1)

            def top8(b, j):
                if late(b, 1):
                    dve.wait_ge(e_ready, b)
                    dve.wait_ge(chosen_done, b)
                dve.wait_ge(lg_ready, b + 1)
                dve.tensor_copy(lg_now[:], LG).then_inc(lg_read, 1)
                wait_alone(dve, lg_read, b + 1)
                dve.max(top_now[:], lg_now[:]).then_inc(top_done, 1)
                wait_alone(dve, top_done, b + 1)
                dve.match_replace(rest_now[:], top_now[:], lg_now[:], LOWEST).then_inc(rest_done, 1)
                dve.tensor_scalar(neg_top[:], top_now[:, 0:1], -1.0, None, ALU.mult).then_inc(neg_done, 1)
                dve.wait_ge(rest_done, b + 1)
                if late(b, 2):
                    dve.wait_ge(rank_ready, b - 1)
                    dve.wait_ge(before_done, b - 1)
                dve.tensor_tensor(chosen[:, j % 2, :], rest_now[:], lg_now[:], ALU.not_equal).then_inc(chosen_done, 1)

            def weigh(b, j):
                dve.wait_ge(e_ready, b + 1)
                dve.wait_ge(chosen_done, b + 1)
                if late(b, 1):
                    dve.wait_ge(row_w, b)
                w = row[:, j % RING, M:M + NE]
                dve.tensor_tensor(picked[:], e_now[:], chosen[:, j % 2, :], ALU.mult).then_inc(picked_done, 1)
                dve.wait_ge(picked_done, b + 1)
                dve.tensor_reduce(wsum[:, 0:1], picked[:], AX.X, ALU.add).then_inc(wsum_done, 1)
                dve.wait_ge(wsum_done, b + 1)
                dve.scalar_tensor_tensor(wsum[:, 1:2], wsum[:, 0:1], 0.0, wsum[:, 0:1],
                                         op0=ALU.is_equal, op1=ALU.add).then_inc(wsum1_done, 1)
                dve.wait_ge(wsum1_done, b + 1)
                dve.reciprocal(wsum[:, 2:3], wsum[:, 1:2]).then_inc(winv_done, 1)
                dve.wait_ge(winv_done, b + 1)
                dve.tensor_scalar(w, picked[:], wsum[:, 2:3], None, ALU.mult).then_inc(row_w, 1)

            def place_wide(b):
                if late(b, 1):
                    dve.wait_ge(slot_masked, b)
                dve.wait_ge(rank_ready, b + 1)
                dve.scalar_tensor_tensor(slot_now[:], RK, float(CAP), first_slot[:],
                                         op0=ALU.min, op1=ALU.add).then_inc(slot_wide, 1)

            def place(b, j):
                if late(b, 1):
                    dve.wait_ge(slots_ready, b)
                    dve.wait_ge(before_done, b)
                dve.wait_ge(slot_wide, b + 1)
                dve.tensor_tensor(slot_masked_t[:], slot_now[:], chosen[:, j % 2, :], ALU.mult
                                  ).then_inc(slot_masked, 1)
                dve.tensor_tensor(before[:, (j + 1) % 2, :], before[:, j % 2, :], chosen[:, j % 2, :], ALU.add
                                  ).then_inc(before_done, 1)
                wait_alone(dve, slot_masked, b + 1)
                dve.max(top_slot[:], slot_masked_t[:]).then_inc(slot_top, 1)
                if late(b, RING):
                    dve.wait_ge(row_sent[j % RING], (b - j % RING) * (K8 * 16 // RING))
                dve.wait_ge(slot_top, b + 1)
                dve.tensor_scalar(slots[:, j % RING, :], top_slot[:], -1.0, None, ALU.add).then_inc(slots_ready, 1)

            for b in range(2):
                ln1(b, b)
                ln1_apply(b, b)
            for b in range(2):
                residual(b, b)
                third_part(b, b)
            for b in range(2, AHEAD):
                ln1(b, b)
                ln1_apply(b, b)
            dve.memset(ys[:], 0.0).then_inc(zeroed, 1)
            for b in range(2, AHEAD):
                residual(b, b)
                third_part(b, b)
            for h in range(H):
                head_max(0, 0, h)
            split_max(0, 0)
            dve.wait_ge(tables, 9)

            def step(b, j):
                nxt, ahead = live(b + 1, NB), live(b + AHEAD, NB)
                y_, s_ = live(b - Y_LAG, NB), live(b - LAG, NB)
                if nxt:
                    head_max(b + 1, j + 1, 0)
                if y_:
                    attend(b - Y_LAG)
                if nxt:
                    head_max(b + 1, j + 1, 1)
                if y_:
                    ln2(b - Y_LAG)
                if nxt:
                    head_max(b + 1, j + 1, 2)
                if s_:
                    place_wide(b - LAG)
                if ahead:
                    ln1(b + AHEAD, j + AHEAD)
                if nxt:
                    head_max(b + 1, j + 1, 3)
                if y_:
                    ln2_apply(b - Y_LAG, j - Y_LAG)
                if ahead:
                    ln1_apply(b + AHEAD, j + AHEAD)
                if nxt:
                    head_max(b + 1, j + 1, 4)
                if s_:
                    weigh(b - LAG, j - LAG)
                if nxt:
                    head_max(b + 1, j + 1, 5)
                if ahead:
                    residual(b + AHEAD, j + AHEAD)
                if s_:
                    place(b - LAG, j - LAG)
                if nxt:
                    head_max(b + 1, j + 1, 6)
                if ahead:
                    third_part(b + AHEAD, j + AHEAD)
                if nxt:
                    head_max(b + 1, j + 1, 7)
                    split_max(b + 1, j + 1)
                if y_:
                    top8(b - Y_LAG, j - Y_LAG)

            steps(dve, step)
            dve.wait_ge(count_ready, 1)
            k = [0]

            def link(ins):
                k[0] += 1
                ins.then_inc(plan_done, 1)
                dve.wait_ge(plan_done, k[0])

            link(dve.tensor_copy(count[:], RK))
            link(dve.tensor_scalar(few[:], count[:], float(P), float(TOK), ALU.is_lt, ALU.mult))
            link(dve.tensor_tensor(few[:], few[:], count[:], ALU.max))
            link(dve.tensor_reduce(most[:], few[:], AX.X, ALU.max))
            link(dve.tensor_copy(most_i[:], most[:]))
            for c in range(1, NC):
                a, n = CT[c]
                link(dve.tensor_scalar(start[:, c, :], count[:], float(a + n), float(-n), ALU.min, ALU.add))
                link(dve.scalar_tensor_tensor(start_f[:], start[:, c, :], -1.0, first_slot[:], op0=ALU.add, op1=ALU.add))
                link(dve.tensor_copy(start_i[:, c - 1, :], start_f[:]))
                if c == 1:
                    link(dve.tensor_scalar(new[:], start[:, c, :], trash[:, 0:1], float(TOK + 1 + P),
                                           ALU.add, ALU.is_ge))
                else:
                    link(dve.tensor_tensor(new[:], start[:, c, :], start[:, c - 1, :], ALU.subtract))
                    link(dve.tensor_scalar(new[:], new[:], trash[:, 0:1], float(TOK + 1 + CT[c - 1][1]),
                                           ALU.add, ALU.is_ge))
                new_c = is_new[:, :, c:c + 1].rearrange("p e o -> p (e o)")
                past_c = past[:, :, c:c + 1].rearrange("p e o -> p (e o)")
                link(dve.tensor_copy(new_c, new[:]))
                link(dve.tensor_scalar(new[:], new[:], -1.0, 1.0, ALU.mult, ALU.add))
                link(dve.tensor_scalar(past_c, new[:], trash[:, 0:1], -1.0, ALU.mult, ALU.add))
            link(dve.memset(is_new[:, :, 0:1], 1.0))
            link(dve.memset(past[:, :, 0:1], -1.0))
            dve.nop(nofuse=True).then_inc(flag_ready, 1)
            busiest = dve.value_load(most_i[0:1, 0:1], min_val=0, max_val=TOK)

            def copy_y(e, j):
                dve.wait_ge(t_ready, e + 1)
                if late(e, 2):
                    dve.wait_ge(gu_ready, e - 1)
                dve.tensor_copy(yT[:, j % 2, 0, :], t_ps[0][:, 0:CAP]).then_inc(yt0, 1)

            def numbers(e, j):
                r = j % RING
                num = rows[:, r, :, ROW - 1:ROW].rearrange("p c o -> p (c o)")
                if late(e, RING):
                    for c in range(NC):
                        dve.wait_ge(added[c], (e - (RING - 1)) * 16)
                else:
                    dve.wait_ge(rows_clear, 1)
                dve.wait_ge(rows_in[r], rounds(e, j, 16 * NC))
                dve.tensor_copy(w3[:, r, :], rows[:, r, :, bass.ds(e + M, 1)].rearrange("p c o -> p (c o)")
                                ).then_inc(w_ready, 1)
                if late(e, 1):
                    dve.wait_ge(to_ready, e)
                dve.tensor_tensor(num_new[:], num, is_new[:, bass.ds(e, 1), :].rearrange("p a c -> p (a c)"),
                                  ALU.mult).then_inc(pad_ready, 1)
                dve.wait_ge(pad_ready, e + 1)
                dve.tensor_tensor(to[:, r, :], num_new[:], past[:, bass.ds(e, 1), :].rearrange("p a c -> p (a c)"),
                                  ALU.add).then_inc(to_ready, 1)

            def hidden(e, j):
                dve.wait_ge(silu_done, e + 1)
                if late(e, 2):
                    dve.wait_ge(down_ready, e * NC - NC)
                dve.tensor_tensor(hT[:, j % 2, :], silu[:, j % 2, :], u_ps[j % 2][0:I, 0:CAP], ALU.mult
                                  ).then_inc(h_ready, 1)

            def weigh_last(e, j):
                a, n = CT[-1]
                dve.wait_ge(down_ready, e * NC + NC)
                dve.wait_ge(w_ready, e + 1)
                dve.tensor_scalar(ys[0:n, j % RING, NC - 1, :], d_ps[NC - 1][0:n], w3[0:n, j % RING, NC - 1:NC],
                                  None, ALU.mult).then_inc(ys2, 1)

            def expert_step(e, j):
                if live(e + 1, NE):
                    numbers(e + 1, j + 1)
                    copy_y(e + 1, j + 1)
                if live(e, NE):
                    hidden(e, j)
                if live(e - 1, NE):
                    weigh_last(e - 1, j - 1)

            with dve.If(busiest < CAP + 1):
                dve.wait_ge(acc_clear, ACC_CLEARS * 16)
                numbers(0, 0)
                copy_y(0, 0)
                expert_steps(dve, expert_step, 1)
                for k in range(NB // FB):
                    n = k % 2
                    dve.wait_ge(fin_in[n], 16 * NC * (k // 2 + 1))
                    for c in range(1, NC):
                        ins = dve.tensor_tensor(fin[:, n, 0], fin[:, n, 0], fin[:, n, c], ALU.add)
                        if c < NC - 1:
                            ins.then_inc(fin_add, 1)
                            dve.wait_ge(fin_add, k + 1)
                    ins.then_inc(fin_ready, 1)
            with dve.Else():
                def up_times_silu(e, c):
                    dve.wait_ge(silu_done_d, e * NCH + (c + 1))
                    dve.tensor_tensor(hT_d[:, c % 2, :], silu_d[:, c % 2, :], ud_ps[c % 2][0:I], ALU.mult
                                      ).then_inc(h_ready_d, 1)

                def accumulate(e, t):
                    dve.wait_ge(down_ready_d, e * NB + (t + 1))
                    if late(e, 1):
                        dve.wait_ge(acc_done_d, e * NB + (t + 1) - NB)
                    dve.scalar_tensor_tensor(X[:, t, :], dd_ps[t % DOWN], w_all[:, t, bass.ds(e, 1)],
                                             X[:, t, :], op0=ALU.mult, op1=ALU.add).then_inc(acc_done_d, 1)

                def expert_d(e):
                    up_times_silu(e, 0)
                    for c in range(1, NCH):
                        up_times_silu(e, c)
                        for t in range((c - 1) * CH // P, c * CH // P):
                            accumulate(e, t)
                    for t in range((NCH - 1) * CH // P, NB):
                        accumulate(e, t)

                dve.wait_ge(x1_kept, 16)
                dve.wait_ge(w_kept, NB)
                expert_d(0)
                with dve.Fori(1, NE) as e:
                    expert_d(e)

        @block.scalar
        def _(act):
            def first_part(b, j):
                act.wait_ge(q_ready, b + 1)
                act.wait_ge(c_in[(j // 2) % 2], rounds(b, j, 16))
                if late(b, RING):
                    act.wait_ge(parts_stored[(j // 2) % 2], (b - j % RING) * 4)
                act.copy(parts[:, (j // 2) % 2, :, 0, j % 2, :], qk[:, j % RING]).then_inc(split_hi, 1)

            def second_part(b, j):
                act.wait_ge(split_res, b + 1)
                act.copy(parts[:, (j // 2) % 2, :, 1, j % 2, :], qk_res[:]).then_inc(split_mid, 1)

            def copy_v(b, j):
                act.wait_ge(v_t, b + 1)
                if isinstance(b, int) and b == 0:
                    act.wait_ge(consts, 14)
                if late(b, RING):
                    act.wait_ge(pv_done, b - (RING - 1))
                for i in range(2):
                    last = act.copy(vT[:, j % RING, :, :, i, i * D:(i + 1) * D],
                                    M0.rearrange("p (t q i d) -> p t q i d", t=MT, q=NPAIR, i=2)[:, :, :, i, :])
                last.then_inc(v_ready, 1)

            def copy_negmax(b, j):
                act.wait_ge(nm_t, b + 1)
                if late(b, 2):
                    act.wait_ge(st_ready, b * NPAIR - NPAIR)
                act.copy(nm_rows[0:PARTS * H, j % 2, :], NM16[0:PARTS * H, :]).then_inc(nm_ready, 1)

            def exps(b, j, pair):
                act.wait_ge(st_ready, b * NPAIR + (pair + 1))
                if pair == 0 and late(b, 2):
                    act.wait_ge(pv_done, b - 1)
                act.activation(pT[:, j % 2, pair], st_ps[:, pair % 2], ACT.Exp, scale=QSCALE).then_inc(exp_done, 1)

            def copy_yT(b):
                act.wait_ge(y_t, b + 1)
                if late(b, 1):
                    act.wait_ge(lg_ready, b)
                act.copy(y_now[:], M0.rearrange("p (t n) -> p t n", t=MT)).then_inc(yt_ready, 1)

            def keep_yT(b):
                act.wait_ge(yt_ready, b + 1)
                act.copy(yT_all[:, :, bass.ds(b * P, P)], y_now[:]).then_inc(yt_kept, 1)

            def number_row(b, j):
                if isinstance(b, int) and b == 0:
                    act.wait_ge(tables, 9)
                if late(b, RING):
                    act.wait_ge(row_sent[j % RING], (b - j % RING) * (K8 * 16 // RING))
                act.copy(row[:, j % RING, ROW - 1:ROW], token[:, bass.ds(b, 1)]).then_inc(row_number, 1)

            def keep_w(b, j):
                act.wait_ge(row_w, b + 1)
                act.copy(w_all[:, bass.ds(b, 1), :].rearrange("p a e -> p (a e)"), row[:, j % RING, M:M + NE]
                         ).then_inc(w_kept, 1)

            def exp_logits(b):
                act.wait_ge(neg_done, b + 1)
                if late(b, 1):
                    act.wait_ge(picked_done, b)
                act.activation(e_now[:], lg_now[:], ACT.Exp, bias=neg_top[:, 0:1]).then_inc(e_ready, 1)

            for b in range(AHEAD):
                first_part(b, b)
                second_part(b, b)
                if b == 1:
                    act.wait_ge(gw_t, 1)
                    act.copy(gwT[:].rearrange("p t e -> p (t e)"), M0[:, 0:MT * NE]).then_inc(gw_ready, 1)
            copy_v(0, 0)
            copy_negmax(0, 0)

            def step(b, j):
                now, nxt, ahead = live(b, NB), live(b + 1, NB), live(b + AHEAD, NB)
                y_, s_ = live(b - Y_LAG, NB), live(b - LAG, NB)
                if now:
                    exps(b, j, 0)
                if s_:
                    exp_logits(b - LAG)
                if now:
                    exps(b, j, 1)
                if nxt:
                    copy_v(b + 1, j + 1)
                if y_:
                    copy_yT(b - Y_LAG)
                if ahead:
                    first_part(b + AHEAD, j + AHEAD)
                if now:
                    exps(b, j, 2)
                if y_:
                    keep_yT(b - Y_LAG)
                    number_row(b - Y_LAG, j - Y_LAG)
                if ahead:
                    second_part(b + AHEAD, j + AHEAD)
                if now:
                    exps(b, j, 3)
                if nxt:
                    copy_negmax(b + 1, j + 1)
                if s_:
                    keep_w(b - LAG, j - LAG)

            steps(act, step)

            def copy_y(e, j):
                act.wait_ge(t_ready, e + 1)
                if late(e, 2):
                    act.wait_ge(gu_ready, e - 1)
                act.copy(yT[:, j % 2, 1, :], t_ps[1][:, 0:CAP]).then_inc(yt1, 1)

            def silu_gate(e, j):
                act.wait_ge(gu_ready, e + 1)
                if late(e, 2):
                    act.wait_ge(h_ready, e - 1)
                act.activation(silu[:, j % 2, :], g_ps[j % 2][0:I, 0:CAP], ACT.Silu).then_inc(silu_done, 1)

            def weigh_first(e, j):
                act.wait_ge(down_ready, e * NC + 2)
                act.wait_ge(w_ready, e + 1)
                if late(e, RING):
                    for c in range(2):
                        act.wait_ge(added[c], (e - (RING - 1)) * 16)
                for c in range(2):
                    last = act.activation(ys[:, j % RING, c, :], d_ps[c], ACT.Copy, scale=w3[:, j % RING, c:c + 1])
                last.then_inc(ys01, 1)

            act.wait_ge(flag_ready, 1)
            busiest = act.value_load(most_i[0:1, 0:1], min_val=0, max_val=TOK)

            def expert_step(e, j):
                if live(e + 1, NE):
                    copy_y(e + 1, j + 1)
                if live(e, NE):
                    silu_gate(e, j)
                if live(e - 1, NE):
                    weigh_first(e - 1, j - 1)

            with act.If(busiest < CAP + 1):
                act.wait_ge(acc_clear, ACC_CLEARS * 16)
                copy_y(0, 0)
                expert_steps(act, expert_step, 1)
            with act.Else():
                def expert_d(e):
                    for c in range(NCH):
                        act.wait_ge(gu_ready_d, e * NCH + (c + 1))
                        if late(e, 1) or c >= 2:
                            act.wait_ge(h_ready_d, e * NCH + (c - 1))
                        act.activation(silu_d[:, c % 2, :], gd_ps[c % 2][0:I], ACT.Silu).then_inc(silu_done_d, 1)

                expert_d(0)
                with act.Fori(1, NE) as e:
                    expert_d(e)

        @block.tensor
        def _(pe):
            pe.wait_ge(consts, 5)
            pe.wait_ge(gw_in, 16)
            for t in range(MT):
                last = pe.transpose(M0[:, t * NE:(t + 1) * NE], gw[:, t * P:(t + 1) * P], ident[0:NE, 0:NE])
            last.then_inc(gw_t, 1)

            def transpose_v(b, j):
                pe.wait_ge(c_in[(j // 2) % 2], rounds(b, j, 16))
                if late(b, LAG + 1):
                    pe.wait_ge(slot_wide, b - LAG)
                elif b >= 1:
                    pe.wait_ge(nm_ready, b)
                else:
                    pe.wait_ge(gw_ready, 1)
                for t in range(MT):
                    last = pe.transpose(M0[:, t * P:(t + 1) * P], qk[:, j % RING, 1, t * P:(t + 1) * P], ident[:])
                last.then_inc(v_t, 1)

            def scores(b, j, h):
                if h == 0:
                    pe.wait_ge(stacks_in[(j // 2) % 2], rounds(b, j, 16 * 2 * PRODUCTS))
                if late(b, 1) or h >= 2:
                    pe.wait_ge(max_done, b * H + (h - 1))
                gp, bb = (j // 2) % 2, j % 2
                for t in range(MT):
                    last = pe.matmul(s_ps[:, h % 2, t, :], q_stack[0:STACK, gp, h, bb, t * P:(t + 1) * P],
                                     k_stack[0:STACK, gp, h, bb, :], start=True, stop=True)
                last.then_inc(s_ready, 1)

            def scores_t(b, j, pair):
                if pair == 0:
                    pe.wait_ge(nm_ready, b + 1)
                if late(b, 1) or pair >= 2:
                    pe.wait_ge(exp_done, b * NPAIR + (pair - 1))
                gp, bb = (j // 2) % 2, j % 2
                for i in range(2):
                    h = 2 * pair + i
                    for t in range(MT):
                        pe.matmul(st_ps[:, pair % 2, i, t, :], k_stack[0:STACK, gp, h, bb, t * P:(t + 1) * P],
                                  q_stack[0:STACK, gp, h, bb, :], start=True, stop=False)
                        last = pe.matmul(st_ps[:, pair % 2, i, t, :], pick[:, h, :],
                                         nm_rows[:, j % 2, :], start=False, stop=True)
                last.then_inc(st_ready, 1)

            def values(b, j):
                pe.wait_ge(exp_done, b * NPAIR + NPAIR)
                pe.wait_ge(v_ready, b + 1)
                if late(b, 1):
                    pe.wait_ge(att_done, b)
                for what in range(2):
                    for i in range(2):
                        for k in range(MT):
                            for pair in range(NPAIR):
                                left = vT[:, j % RING, k, pair, i, :] if what == 0 else ones[:, i, :]
                                last = pe.matmul(o_ps[QUAD * pair:QUAD * (pair + 1), what, :], left,
                                                 pT[:, j % 2, pair, i, k, :],
                                                 start=(i == 0 and k == 0), stop=(i == 1 and k == MT - 1),
                                                 tile_position=(0, QUAD * pair))
                last.then_inc(pv_done, 1)

            def transpose_y(b, j):
                pe.wait_ge(y_ready, b + 1)
                if live(b + Y_LAG + 1, NB):
                    pe.wait_ge(v_ready, b + (Y_LAG + 2))
                else:
                    pe.wait_ge(slot_wide, b)
                for t in range(MT):
                    last = pe.transpose(M0[:, t * P:(t + 1) * P], row[:, j % RING, t * P:(t + 1) * P], ident[:])
                last.then_inc(y_t, 1)

            def gate(b):
                pe.wait_ge(yt_ready, b + 1)
                for t in range(MT):
                    last = pe.matmul(LG, y_now[:, t, :], gwT[:, t, :], start=(t == 0), stop=(t == MT - 1))
                last.then_inc(lg_ready, 1)

            def rank(b, j):
                pe.wait_ge(chosen_done, b + 1)
                if late(b, 1):
                    pe.wait_ge(before_done, b)
                else:
                    pe.wait_ge(tables, 9)
                if live(b + LAG, NB):
                    pe.wait_ge(nm_ready, b + (LAG + 1))
                pe.matmul(RK, lower[:], chosen[:, j % 2, :], start=True, stop=False)
                pe.matmul(RK, ones16[:], before[:, j % 2, :], start=False, stop=True).then_inc(rank_ready, 1)

            def transpose_negmax(b, j):
                pe.wait_ge(nm_split, b + 1)
                if late(b, LAG):
                    pe.wait_ge(lg_read, b - (LAG - 1))
                else:
                    pe.wait_ge(v_ready, b + 1)
                for t in range(MT):
                    last = pe.transpose(NM16[0:PARTS * H, t * P:(t + 1) * P],
                                        nm_parts[:, j % 2, t].rearrange("p t h -> p (t h)"), ident16[:])
                last.then_inc(nm_t, 1)

            transpose_v(0, 0)
            for h in range(H):
                scores(0, 0, h)
            transpose_negmax(0, 0)
            pe.wait_ge(consts, 14)

            def step(b, j):
                now, nxt = live(b, NB), live(b + 1, NB)
                y_, s_ = live(b - Y_LAG, NB), live(b - LAG, NB)
                if nxt:
                    scores(b + 1, j + 1, 0)
                    scores(b + 1, j + 1, 1)
                if now:
                    scores_t(b, j, 0)
                if s_:
                    rank(b - LAG, j - LAG)
                if nxt:
                    scores(b + 1, j + 1, 2)
                if now:
                    scores_t(b, j, 1)
                if nxt:
                    transpose_v(b + 1, j + 1)
                    scores(b + 1, j + 1, 3)
                    scores(b + 1, j + 1, 4)
                if y_:
                    transpose_y(b - Y_LAG, j - Y_LAG)
                if now:
                    scores_t(b, j, 2)
                if nxt:
                    scores(b + 1, j + 1, 5)
                    scores(b + 1, j + 1, 6)
                if y_:
                    gate(b - Y_LAG)
                if now:
                    scores_t(b, j, 3)
                if nxt:
                    scores(b + 1, j + 1, 7)
                if live(b - 1, NB):
                    values(b - 1, j - 1)
                if nxt:
                    transpose_negmax(b + 1, j + 1)

            steps(pe, step)
            pe.wait_ge(before_done, NB)
            pe.wait_ge(slot_wide, NB)
            pe.matmul(RK, ones16[:], before[:, NB % 2, :], start=True, stop=True).then_inc(count_ready, 1)
            pe.wait_ge(flag_ready, 1)
            busiest = pe.value_load(most_i[0:1, 0:1], min_val=0, max_val=TOK)

            def transpose_rows(e, j):
                pe.wait_ge(rows_in[j % RING], rounds(e, j, 16 * NC))
                if late(e, 1):
                    pe.wait_ge(yt0, e)
                    pe.wait_ge(yt1, e)
                for t in range(MT):
                    for c, (a, n) in enumerate(CT):
                        last = pe.transpose(t_ps[t][:, a:a + n], rows[0:n, j % RING, c, t * P:(t + 1) * P],
                                            ident[0:n, 0:n])
                last.then_inc(t_ready, 1)

            def gate_up(e, j):
                pe.wait_ge(weights_in[j % RING], rounds(e, j, 32))
                pe.wait_ge(yt0, e + 1)
                pe.wait_ge(yt1, e + 1)
                if late(e, 2):
                    pe.wait_ge(h_ready, e - 1)
                for half, banks in enumerate((g_ps, u_ps)):
                    for t in range(MT):
                        last = pe.matmul(banks[j % 2][0:I, 0:CAP], wgu[:, j % RING, t, half * I:(half + 1) * I],
                                         yT[:, j % 2, t, :], start=(t == 0), stop=(t == MT - 1))
                last.then_inc(gu_ready, 1)

            def down(e, j):
                pe.wait_ge(h_ready, e + 1)
                for c, (a, n) in enumerate(CT):
                    if late(e, 1) and c == 0:
                        pe.wait_ge(ys01, e)
                    if late(e, 1) and c == NC - 1:
                        pe.wait_ge(ys2, e)
                    pe.matmul(d_ps[c][0:n], hT[:, j % 2, a:a + n], wd[:, j % RING, :],
                              start=True, stop=True).then_inc(down_ready, 1)

            def expert_step(e, j):
                if live(e + 1, NE):
                    transpose_rows(e + 1, j + 1)
                if live(e, NE):
                    gate_up(e, j)
                if live(e - 1, NE):
                    down(e - 1, j - 1)

            with pe.If(busiest < CAP + 1):
                transpose_rows(0, 0)
                expert_steps(pe, expert_step, 1)
            with pe.Else():
                def gate_up_d(e, w, c):
                    n = c % 2
                    if c == 0:
                        pe.wait_ge(dense_in[w], (e + (2 - w)) * 16)
                    if late(e, 1) or c >= 2:
                        pe.wait_ge(h_ready_d, e * NCH + (c - 1))
                    for half, banks in enumerate((gd_ps, ud_ps)):
                        for t in range(MT):
                            last = pe.matmul(banks[n][0:I], wgu[:, w, t, half * I:(half + 1) * I],
                                             yT_all[:, t, c * CH:(c + 1) * CH], start=(t == 0), stop=(t == MT - 1))
                    last.then_inc(gu_ready_d, 1)

                def down_d(e, w, c):
                    pe.wait_ge(h_ready_d, e * NCH + (c + 1))
                    for i in range(CH // P):
                        t = c * CH // P + i
                        if late(e, 1) or t >= DOWN:
                            pe.wait_ge(acc_done_d, e * NB + (t + 1 - DOWN))
                        pe.matmul(dd_ps[t % DOWN], hT_d[:, c % 2, i * P:(i + 1) * P], wd[:, w, :],
                                  start=True, stop=True).then_inc(down_ready_d, 1)

                def expert_d(e, w):
                    gate_up_d(e, w, 0)
                    for c in range(1, NCH):
                        gate_up_d(e, w, c)
                        down_d(e, w, c - 1)
                    down_d(e, w, NCH - 1)

                pe.wait_ge(yt_kept, NB)
                expert_d(0, 0)
                expert_d(1, 1)
                with pe.Fori(1, NE // 2) as i:
                    for w in range(2):
                        expert_d(i * 2 + w, w)



_INS = ['x', 'ctx_2048', 'L0_ffn_gate_weight', 'L0_ffn_gate_up_weights', 'L0_ffn_down_weights']


def kernel(**inputs):
    import numpy as _np
    import concourse.bacc as _bacc
    from concourse import mybir as _mybir
    from concourse.bass_utils import run_bass_kernel_spmd as _run

    nc = _bacc.Bacc("TRN2", target_bir_lowering=False, num_devices=1)
    arrays, args = {}, []
    for name in _INS:
        a = _np.ascontiguousarray(inputs[name])
        arrays[f"in_{name}"] = a
        args.append(nc.dram_tensor(f"in_{name}", a.shape, _mybir.dt.from_np(a.dtype), kind="ExternalInput").ap())
    args.append(nc.dram_tensor("out_dram", inputs["x"].shape, F32, kind="ExternalOutput").ap())
    build(nc, *args)
    r = _run(nc, [arrays], core_ids=[0])
    return r.results[0]["out_dram"]
```

```python
from contextlib import ExitStack

import concourse.bass as bass
from concourse import mybir

F32 = mybir.dt.float32
BF16 = mybir.dt.bfloat16
I32 = mybir.dt.int32
ALU = mybir.AluOpType
ACT = mybir.ActivationFunctionType
AX = mybir.AxisListType

P = 128
EPS = 1e-5
LOWEST = -3.0e38
PARTS = 3
PRODUCTS = 6
RING = 4
CAP = 352


def tiles_of(n):
    return [(a, min(P, n - a)) for a in range(0, n, P)]


def build(nc, x, ctx_in, gate_w, gate_up_w, down_w, out):
    NB, ROWS, M = x.shape
    H = 8
    D = ROWS // H
    MT = M // P
    NE = gate_w.shape[0]
    I2 = gate_up_w.shape[2]
    I = I2 // 2
    K8 = 8
    TOK = NB * ROWS
    QSCALE = float(D) ** -0.5
    STACK = PRODUCTS * D
    NPAIR = H // 2
    NG = NB // 2
    AHEAD = 4
    Y_LAG = 2
    LAG = 3
    SEND_LAG = 4
    V_AHEAD = 2
    QUAD = 32
    CT = tiles_of(CAP)
    NC = len(CT)
    SLOTS = CAP + 2
    ACCS = 2
    ROW = M + NE + 1
    XROWS = NE * SLOTS
    CH = 512
    NCH = TOK // CH


    def live(n, count):
        return not isinstance(n, int) or 0 <= n < count

    def late(n, first):
        return not isinstance(n, int) or n >= first

    with ExitStack() as es:
        def sb(name, shape, dt=F32):
            return es.enter_context(nc.sbuf_tensor(name, shape, dt))

        def ps(name, shape, dt=F32):
            return es.enter_context(nc.psum_tensor(name, shape, dt))

        def sem(name):
            return es.enter_context(nc.semaphore(name))

        def sems(name, n):
            return [sem(f"{name}{i}") for i in range(n)]

        X = sb("X", [P, NB, M])
        qk = sb("qk", [P, RING, 2, M])
        qk_res = sb("qk_res", [P, 2, M])
        parts = sb("parts", [P, 2, 2, PARTS, 2, M], BF16)
        q_stack = sb("q_stack", [P, 2, H, 2, M], BF16)
        k_stack = sb("k_stack", [P, 2, H, 2, M], BF16)
        vT = sb("vT", [P, RING, MT, NPAIR, 2, QUAD])
        ones = sb("ones", [P, 2, QUAD])
        pT = sb("pT", [P, 2, NPAIR, 2, MT, M])
        negmax = sb("negmax", [P, 2, H, MT])
        nm_res = sb("nm_res", [P, H, MT])
        nm_parts = sb("nm_parts", [P, 2, MT, PARTS, H], BF16)
        nm_rows = sb("nm_rows", [STACK, 2, M], BF16)
        pick = sb("pick", [STACK, H, P], BF16)
        att = sb("att", [P, M])
        share = sb("share", [P, M])
        stats1 = sb("stats1", [P, 6])
        mv1 = sb("mv1", [P, 2, 2])
        rstd1 = sb("rstd1", [P, 2, 2])
        stats2 = sb("stats2", [P, 6])
        mv2 = sb("mv2", [P, 2])
        rstd2 = sb("rstd2", [P, 2])
        minus_half = sb("minus_half", [P, 1])
        ident = sb("ident", [P, P])
        ident16 = sb("ident16", [P, P], BF16)
        gw = sb("gw", [NE, M])
        gwT = sb("gwT", [P, MT, NE])
        y_now = sb("y_now", [P, MT, P])
        row = sb("row", [P, RING, ROW])
        yT_all = sb("yT_all", [P, MT, TOK])
        w_all = sb("w_all", [P, NB, NE])
        lg_now = sb("lg_now", [P, NE])
        top_now = sb("top_now", [P, K8])
        neg_top = sb("neg_top", [P, 1])
        rest_now = sb("rest_now", [P, NE])
        e_now = sb("e_now", [P, NE])
        chosen = sb("chosen", [P, 2, NE], BF16)
        before = sb("before", [P, 2, NE], BF16)
        lower = sb("lower", [P, P], BF16)
        ones16 = sb("ones16", [P, P], BF16)
        first_slot = sb("first_slot", [P, NE])
        slot_now = sb("slot_now", [P, NE])
        picked = sb("picked", [P, NE])
        slot_masked_t = sb("slot_masked_t", [P, NE])
        wsum = sb("wsum", [P, 4])
        top_slot = sb("top_slot", [P, K8])
        slots = sb("slots", [P, RING, K8], I32)
        number = sb("number", [P, NE], I32)
        token_i = sb("token_i", [P, NB], I32)
        token = sb("token", [P, NB])
        trash = sb("trash", [P, NC])
        count = sb("count", [P, NE])
        few = sb("few", [P, NE])
        most = sb("most", [P, 1])
        start = sb("start", [P, NC, NE])
        start_f = sb("start_f", [P, NE])
        start_i = sb("start_i", [P, NC - 1, NE], I32)
        new = sb("new", [P, NE])
        is_new = sb("is_new", [P, NE, NC])
        past = sb("past", [P, NE, NC])
        most_i = sb("most_i", [P, 1], I32)
        wgu = sb("wgu", [P, RING, MT, I2])
        wd = sb("wd", [I, RING, M])
        rows = sb("rows", [P, RING, NC, ROW])
        yT = sb("yT", [P, 2, MT, CAP])
        silu = sb("silu", [I, 2, CAP])
        hT = sb("hT", [I, 2, CAP])
        w3 = sb("w3", [P, RING, NC])
        num_new = sb("num_new", [P, NC])
        to = sb("to", [P, RING, NC], I32)
        ys = sb("ys", [P, RING, NC, M])

        parts_dram = nc.dram_tensor("parts_dram", [NG, 2, PARTS, H, D, 2, M], BF16).ap()
        xg = nc.dram_tensor("rows_by_expert", [XROWS, ROW], F32).ap()
        acc = [nc.dram_tensor(f"acc{i}", [TOK + NC * P, M], F32).ap() for i in range(ACCS)]

        s_ps = ps("s_ps", [P, 2, MT, M])
        st_ps = ps("st_ps", [P, 2, 2, MT, M])
        o_ps = ps("o_ps", [P, 2, M])
        m_ps = ps("m_ps", [P, 2 * M])
        M0 = m_ps[:, 0:M]
        LG = m_ps[:, 0:NE]
        NM16 = m_ps[:, 0:P].bitcast(BF16)
        t_ps = [st_ps[:, 0, t].rearrange("p t m -> p (t m)") for t in range(MT)]
        g_ps = [s_ps[:, n].rearrange("p t m -> p (t m)") for n in range(2)]
        u_ps = [st_ps[:, 1, n].rearrange("p t m -> p (t m)") for n in range(2)]
        d_ps = [o_ps[:, 0, :], o_ps[:, 1, :], m_ps[:, 0:M]]

        pT_flat = pT[:].rearrange("p a b c d m -> p (a b c d m)")
        silu_d = pT_flat[0:I, 0:2 * CH].rearrange("p (n c) -> p n c", n=2)
        hT_d = pT_flat[0:I, 2 * CH:4 * CH].rearrange("p (n c) -> p n c", n=2)
        gd_ps = [st_ps[:, 0, n].rearrange("p t m -> p (t m)") for n in range(2)]
        ud_ps = [st_ps[:, 1, n].rearrange("p t m -> p (t m)") for n in range(2)]
        dd_ps = [s_ps[:, 0, 0, :], s_ps[:, 1, 0, :], o_ps[:, 0, :], M0]
        DOWN = len(dd_ps)
        FB = 4
        fin = pT_flat[:, 0:NB * ACCS * M].rearrange("p (n c b m) -> p n c b m", n=NB // FB, c=ACCS, b=FB)
        RK = m_ps[:, 0:NE]
        ACC_CLEARS = (ACCS - 1) * len(range(0, (TOK + NC * P) * M // P, RING * NC * M)) + 1
        zeros = ys[:].rearrange("p r c m -> p (r c m)")
        ZW = RING * NC * M

        row_free = sem("row_free")
        ys_free = sem("ys_free")
        before_done = sem("before_done")
        gw_in = sem("gw_in")
        consts = sem("consts")
        zeroed = sem("zeroed")
        rows_clear = sem("rows_clear")
        tables = sem("tables")
        gw_t = sem("gw_t")
        gw_ready = sem("gw_ready")
        ln1_stats = sem("ln1_stats")
        ln1_aggr = sem("ln1_aggr")
        ln1_var = sem("ln1_var")
        ln1_rstd = sem("ln1_rstd")
        q_ready = sem("q_ready")
        split_hi = sem("split_hi")
        split_res = sem("split_res")
        split_mid = sem("split_mid")
        parts_ready = sem("parts_ready")
        s_ready = sem("s_ready")
        max_done = sem("max_done")
        nm_hi = sem("nm_hi")
        nm_r = sem("nm_r")
        nm_mid = sem("nm_mid")
        nm_split = sem("nm_split")
        nm_t = sem("nm_t")
        nm_ready = sem("nm_ready")
        v_t = sem("v_t")
        v_ready = sem("v_ready")
        st_ready = sem("st_ready")
        exp_done = sem("exp_done")
        pv_done = sem("pv_done")
        recip_done = sem("recip_done")
        att_done = sem("att_done")
        x1_done = sem("x1_done")
        ln2_stats = sem("ln2_stats")
        ln2_aggr = sem("ln2_aggr")
        ln2_var = sem("ln2_var")
        ln2_rstd = sem("ln2_rstd")
        y_ready = sem("y_ready")
        y_t = sem("y_t")
        yt_ready = sem("yt_ready")
        yt_kept = sem("yt_kept")
        row_number = sem("row_number")
        w_kept = sem("w_kept")
        lg_ready = sem("lg_ready")
        lg_read = sem("lg_read")
        top_done = sem("top_done")
        neg_done = sem("neg_done")
        rest_done = sem("rest_done")
        chosen_done = sem("chosen_done")
        e_ready = sem("e_ready")
        picked_done = sem("picked_done")
        wsum_done = sem("wsum_done")
        guard_done = sem("guard_done")
        wsum1_done = sem("wsum1_done")
        winv_done = sem("winv_done")
        row_w = sem("row_w")
        rank_ready = sem("rank_ready")
        slot_wide = sem("slot_wide")
        slot_masked = sem("slot_masked")
        slot_top = sem("slot_top")
        slots_ready = sem("slots_ready")
        acc_clear = sem("acc_clear")
        x1_kept = sem("x1_kept")
        count_ready = sem("count_ready")
        plan_done = sem("plan_done")
        flag_ready = sem("flag_ready")
        t_ready = sem("t_ready")
        yt0 = sem("yt0")
        yt1 = sem("yt1")
        gu_ready = sem("gu_ready")
        silu_done = sem("silu_done")
        h_ready = sem("h_ready")
        down_ready = sem("down_ready")
        ys01 = sem("ys01")
        ys2 = sem("ys2")
        w_ready = sem("w_ready")
        pad_ready = sem("pad_ready")
        to_ready = sem("to_ready")
        gu_ready_d = sem("gu_ready_d")
        silu_done_d = sem("silu_done_d")
        h_ready_d = sem("h_ready_d")
        down_ready_d = sem("down_ready_d")
        acc_done_d = sem("acc_done_d")
        fin_ready = sem("fin_ready")
        out_in = sem("out_in")
        x_in = sems("x_in", 2)
        c_in = sems("c_in", 2)
        parts_stored = sems("parts_stored", 2)
        stacks_in = sems("stacks_in", 2)
        row_sent = sems("row_sent", RING)
        rows_in = sems("rows_in", RING)
        weights_in = sems("weights_in", RING)
        added = sems("added", ACCS)
        fin_in = sems("fin_in", NB // FB)
        dense_in = sems("dense_in", 2)

        block = es.enter_context(nc.Block())

        xv = x.rearrange("b p m -> p b m")
        cv = ctx_in.rearrange("b p m -> p b m")
        ov = out.rearrange("b p m -> p b m")

        def wait_alone(eng, semaphore, value):
            eng.wait_ge(semaphore, value)
            if not isinstance(value, int):
                eng.nop(nofuse=True)

        def ring_steps(eng, body, count, tail):
            for b in range(RING):
                body(b, b)
            with eng.Fori(1, count // RING - 1) as i:
                for j in range(RING):
                    body(i * RING + j, j)
            for b in range(count - RING, count + tail):
                body(b, b)

        def steps(eng, body):
            ring_steps(eng, body, NB, LAG)

        def expert_steps(eng, body, tail):
            ring_steps(eng, body, NE, tail)

        def rounds(n, j, each):
            return (n + (RING - j % RING)) * (each // RING)

        @block.sync
        def _(sp):
            def load_ctx(g, gp):
                if late(g, 2):
                    sp.wait_ge(v_t, g * 2 - 2)
                    wait_alone(sp, split_res, g * 2 - 2)
                sp.dma_start(qk[:, 2 * gp:2 * gp + 2, 1, :], cv[:, bass.ds(g * 2, 2), :]).then_inc(c_in[gp], 16)

            def stack_group(g, gp, more=False):
                wait_alone(sp, parts_ready, g * 2 + 2)
                sp.dma_start(parts_dram[bass.ds(g, 1)].rearrange("a k t h d b m -> (h d) (a k t) (b m)"),
                             parts[:, gp].rearrange("p k t b m -> p (k t) (b m)")).then_inc(parts_stored[gp], 16)
                if more:
                    load_ctx(g + 1, 1 - gp)
                wait_alone(sp, parts_stored[gp], (g + (2 - gp)) * 8)
                if late(g, 2):
                    wait_alone(sp, st_ready, (g * 2 - 2) * NPAIR)
                row0 = 0
                for a in range(PARTS):
                    n = PARTS - a
                    for t in range(n):
                        src = parts_dram[bass.ds(g, 1), 1, t].rearrange("a h d b m -> d (a h) (b m)")
                        sp.dma_start(k_stack[row0 + t * D:row0 + (t + 1) * D, gp].rearrange("p h b m -> p h (b m)"),
                                     src).then_inc(stacks_in[gp], 16)
                    for t in range(n):
                        src = parts_dram[bass.ds(g, 1), 0, a].rearrange("a h d b m -> d (a h) (b m)")
                        sp.dma_start(q_stack[row0:row0 + D, gp].rearrange("p h b m -> p h (b m)"),
                                     src).then_inc(stacks_in[gp], 16)
                        row0 += D

            load_ctx(0, 0)
            sp.dma_start(X[:, 0:2, :], xv[:, 0:2, :]).then_inc(x_in[0], 16)
            sp.dma_start(gw[:, :], gate_w).then_inc(gw_in, 16)
            load_ctx(1, 1)
            sp.dma_start(X[:, 2:NB, :], xv[:, 2:NB, :]).then_inc(x_in[1], 16)
            stack_group(0, 0)
            zero_pieces = [(acc[0][TOK:TOK + NC * P, :].rearrange("n m -> (n m)").rearrange("(p f) -> p f", p=P),
                            zeros[:, 0:NC * M])]
            for c in range(1, ACCS):
                flat = acc[c].rearrange("n m -> (n m)").rearrange("(p f) -> p f", p=P)
                for a in range(0, (TOK + NC * P) * M // P, ZW):
                    w = min(ZW, (TOK + NC * P) * M // P - a)
                    zero_pieces.append((flat[:, a:a + w], zeros[:, 0:w]))

            def clear(n):
                for _ in range(n):
                    to_, from_ = zero_pieces.pop()
                    sp.dma_start(to_, from_).then_inc(acc_clear, 16)

            stack_group(1, 1, True)
            sp.wait_ge(zeroed, 1)
            clear(1)
            stack_group(2, 0, True)
            clear(1)
            stack_group(3, 1, True)
            clear(1)
            with sp.Fori(2, NG // 2 - 1) as i:
                for gp in range(2):
                    stack_group(i * 2 + gp, gp, True)
            stack_group(NG - 2, 0, True)
            stack_group(NG - 1, 1)
            for b0, b1 in ((0, NB - 3), (NB - 3, NB)):
                sp.wait_ge(x1_done, b1)
                sp.dma_start(acc[0][b0 * P:b1 * P, :].rearrange("(b p) m -> p b m", p=P), X[:, b0:b1, :]
                             ).then_inc(x1_kept, 16)

            def load_rows(e, j):
                r = j % RING
                if late(e, RING):
                    wait_alone(sp, t_ready, e - (RING - 1))
                    wait_alone(sp, to_ready, e - (RING - 1))
                for c, (a, n) in enumerate(CT):
                    if c == 0:
                        first = e * SLOTS
                    else:
                        first = sp.value_load(start_i[0:1, c - 1, bass.ds(e, 1)], min_val=0, max_val=XROWS - P)
                    sp.dma_start(rows[0:n, r, c, :], xg[bass.ds(first, n), :]).then_inc(rows_in[r], 16)

            def load_weights(e, j):
                r = j % RING
                if late(e, RING):
                    wait_alone(sp, down_ready, e * NC - (RING - 1) * NC)
                sp.dma_start(wgu[:, r], gate_up_w[bass.ds(e, 1)].rearrange("a (t p) n -> p (a t) n", p=P)
                             ).then_inc(weights_in[r], 16)
                sp.dma_start(wd[:, r, :], down_w[bass.ds(e, 1)].rearrange("a i m -> i (a m)")
                             ).then_inc(weights_in[r], 16)

            def load_step(e, j):
                if live(e + 1, NE):
                    load_rows(e + 1, j + 1)
                if late(e, RING):
                    load_weights(e, j)

            for e in range(RING):
                load_weights(e, e)
            sp.wait_ge(flag_ready, 1)
            busiest = sp.value_load(most_i[0:1, 0:1], min_val=0, max_val=TOK)
            with sp.If(busiest < CAP + 1):
                for n in range(RING):
                    sp.wait_ge(row_sent[n], NB // RING * K8 * 16)
                sp.wait_ge(rows_clear, 1)
                load_rows(0, 0)
                expert_steps(sp, load_step, 0)

                for c in range(ACCS):
                    sp.wait_ge(added[c], NE // ACCS * NC * 16)
                for k in range(NB // FB):
                    for c in range(ACCS):
                        sp.dma_start(fin[:, k, c],
                                     acc[c][k * FB * P:(k + 1) * FB * P, :].rearrange("(b p) m -> p b m", p=P)
                                     ).then_inc(fin_in[k], 16)
                for k in range(NB // FB):
                    sp.wait_ge(fin_ready, k + 1)
                    sp.dma_start(ov[:, k * FB:(k + 1) * FB, :], fin[:, k, 0]).then_inc(out_in, 16)
                sp.wait_ge(out_in, 16 * (NB // FB))
            with sp.Else():
                def load_dense(e, w):
                    if late(e, 2):
                        wait_alone(sp, down_ready_d, (e - 1) * NB)
                    sp.dma_start(wgu[:, w], gate_up_w[bass.ds(e, 1)].rearrange("a (t p) n -> p (a t) n", p=P)
                                 ).then_inc(dense_in[w], 16)
                    sp.dma_start(wd[:, w, :], down_w[bass.ds(e, 1)].rearrange("a i m -> i (a m)")
                                 ).then_inc(dense_in[w], 16)

                for n in range(RING):
                    sp.wait_ge(weights_in[n], 32)
                load_dense(0, 0)
                load_dense(1, 1)
                with sp.Fori(1, NE // 2) as i:
                    for w in range(2):
                        load_dense(i * 2 + w, w)
                sp.wait_ge(acc_done_d, NE * NB)
                sp.dma_start(ov, X[:, :, :]).then_inc(out_in, 16)
                sp.wait_ge(out_in, 16)
            sp.wait_ge(x1_kept, 32)
            sp.wait_ge(acc_clear, 16 * ACC_CLEARS)
            for n in range(RING):
                sp.wait_ge(row_sent[n], NB // RING * K8 * 16)

        @block.gpsimd
        def _(pool):
            pool.nop(nofuse=True).then_inc(row_free, RING)
            pool.nop(nofuse=True).then_inc(ys_free, RING)
            pool.memset(ident[:], 0.0).then_inc(consts, 1)
            pool.memset(ident16[:], 0.0).then_inc(consts, 1)
            pool.memset(minus_half[:], -0.5).then_inc(consts, 1)
            pool.wait_ge(consts, 3)
            for m in (ident, ident16):
                pool.affine_select(out=m[:], in_=m[:], compare_op=ALU.not_equal, fill=1.0, base=0,
                                   pattern=[[-1, P]], channel_multiplier=1).then_inc(consts, 1)

            def rstd(sem_in, sem_var, sem_out, b, mv, out_):
                wait_alone(pool, sem_in, b + 1)
                pool.tensor_scalar(out_[:, 0:1], mv[:, 1:2], EPS, None, ALU.add).then_inc(sem_var, 1)
                pool.wait_ge(sem_var, b + 1)
                pool.tensor_tensor(out_[:, 1:2], out_[:, 0:1], minus_half[:], ALU.pow).then_inc(sem_out, 1)

            def rstd_1(b, j):
                rstd(ln1_aggr, ln1_var, ln1_rstd, b, mv1[:, j % 2], rstd1[:, j % 2])

            def third_part(b, j):
                pool.wait_ge(split_mid, b + 1)
                pool.tensor_tensor(parts[:, (j // 2) % 2, :, 2, j % 2, :], qk_res[:],
                                   parts[:, (j // 2) % 2, :, 1, j % 2, :], ALU.subtract).then_inc(parts_ready, 1)

            pool.memset(vT[:], 0.0).then_inc(consts, 1)
            pool.memset(ones[:], 0.0).then_inc(consts, 1)
            pool.wait_ge(consts, 7)
            for i in range(2):
                pool.memset(ones[:, i, i * D:(i + 1) * D], 1.0).then_inc(consts, 1)
            for b in range(2):
                rstd_1(b, b)
            for b in range(2):
                third_part(b, b)
            for b in range(2, AHEAD):
                rstd_1(b, b)
            pool.memset(pick[:], 0.0).then_inc(consts, 1)
            pool.memset(nm_rows[:], 0.0).then_inc(consts, 1)
            for t in range(PARTS):
                pool.wait_ge(consts, 11 + t)
                pool.affine_select(out=pick[:], in_=pick[:], compare_op=ALU.not_equal, fill=1.0,
                                   base=-t * H, pattern=[[-1, H], [0, P]],
                                   channel_multiplier=1).then_inc(consts, 1)
            for b in range(2, AHEAD):
                third_part(b, b)
            pool.memset(ones16[:], 1.0).then_inc(tables, 1)
            pool.memset(before[:], 0.0).then_inc(tables, 1)
            pool.iota(token_i[:], pattern=[[P, NB]], base=1, channel_multiplier=1).then_inc(tables, 1)
            pool.iota(number[:], pattern=[[SLOTS, NE]], base=1, channel_multiplier=0).then_inc(tables, 1)
            pool.wait_ge(tables, 4)
            pool.affine_select(out=lower[:], in_=ones16[:], compare_op=ALU.is_gt, fill=0.0, base=0,
                               pattern=[[1, P]], channel_multiplier=-1).then_inc(tables, 1)
            pool.tensor_copy(token[:], token_i[:]).then_inc(tables, 1)
            pool.tensor_copy(first_slot[:], number[:]).then_inc(tables, 1)
            pool.wait_ge(tables, 7)
            pool.iota(number[:, 0:NC], pattern=[[P, NC]], base=TOK + 1, channel_multiplier=1).then_inc(tables, 1)
            pool.wait_ge(tables, 8)
            pool.tensor_copy(trash[:], number[:, 0:NC]).then_inc(tables, 1)
            pool.memset(ys[:], 0.0).then_inc(zeroed, 1)
            pool.memset(rows[:], 0.0).then_inc(rows_clear, 1)

            def send(b, j, part):
                pool.wait_ge(row_number, b + 1)
                pool.wait_ge(w_kept, b + 1)
                pool.wait_ge(row_w, b + 1)
                wait_alone(pool, slots_ready, b + 1)
                for k in (range(0, 2), range(2, 6), range(6, K8))[part]:
                    pool.indirect_dma_start(xg, bass.IndirectOffsetOnAxis(ap=slots[:, j % RING, k:k + 1], axis=0),
                                            row[:, j % RING, :], None).then_inc(row_sent[j % RING], 16)

            def landed(b, j):
                if not (isinstance(b, int) and b >= NB - RING):
                    wait_alone(pool, row_sent[j % RING], rounds(b, j, K8 * 16))
                    pool.nop(nofuse=True).then_inc(row_free, 1)

            def step(b, j):
                sending, ahead = live(b - SEND_LAG, NB), live(b + AHEAD, NB)
                if live(b - Y_LAG, NB) and not live(b, NB):
                    rstd(ln2_aggr, ln2_var, ln2_rstd, b - Y_LAG, mv2, rstd2)
                if sending:
                    send(b - SEND_LAG, j - SEND_LAG, 0)
                if j % RING != 0 and sending:
                    landed(b - SEND_LAG - 1, j - 1)
                if ahead:
                    rstd_1(b + AHEAD, j + AHEAD)
                if live(b - Y_LAG, NB) and live(b, NB):
                    rstd(ln2_aggr, ln2_var, ln2_rstd, b - Y_LAG, mv2, rstd2)
                if sending:
                    send(b - SEND_LAG, j - SEND_LAG, 1)
                if ahead:
                    third_part(b + AHEAD, j + AHEAD)
                if sending:
                    send(b - SEND_LAG, j - SEND_LAG, 2)
                if j % RING == RING - 1 and sending:
                    landed(b - SEND_LAG, j)

            ring_steps(pool, step, NB, SEND_LAG)

            def add_rows(e, j):
                r = j % RING
                wait_alone(pool, to_ready, e + 1)
                if late(e, ACCS):
                    wait_alone(pool, added[j % ACCS], (e - j % ACCS) * (NC * 16 // ACCS))
                    pool.nop(nofuse=True).then_inc(ys_free, 1)
                for c, (a, n) in enumerate(CT):
                    if c == 0:
                        wait_alone(pool, ys01, e + 1)
                    if c == NC - 1:
                        wait_alone(pool, ys2, e + 1)
                    pool.indirect_dma_start(acc[j % ACCS], bass.IndirectOffsetOnAxis(ap=to[0:n, r, c:c + 1], axis=0),
                                            ys[0:n, r, c, :], None, compute_op=ALU.add
                                            ).then_inc(added[j % ACCS], 16)

            pool.wait_ge(flag_ready, 1)
            busiest = pool.value_load(most_i[0:1, 0:1], min_val=0, max_val=TOK)
            with pool.If(busiest < CAP + 1):
                pool.wait_ge(acc_clear, ACC_CLEARS * 16)
                pool.wait_ge(x1_kept, 32)
                expert_steps(pool, lambda e, j: add_rows(e, j) if live(e, NE) else None, 0)

        @block.vector
        def _(dve):
            def batch(t, b):
                return t[:, bass.ds(b, 1), :].rearrange("p a m -> p (a m)")

            def ln1(b, j):
                if isinstance(b, int):
                    dve.wait_ge(x_in[0 if b < 2 else 1], 16)
                if late(b, 1):
                    wait_alone(dve, ln1_aggr, b)
                dve.bn_stats(stats1[:], batch(X, b)).then_inc(ln1_stats, 1)
                if late(b, 2):
                    dve.wait_ge(q_ready, b - 1)
                wait_alone(dve, ln1_stats, b + 1)
                dve.bn_aggr(mv1[:, j % 2, :], stats1[:]).then_inc(ln1_aggr, 1)

            def ln1_apply(b, j):
                dve.wait_ge(ln1_rstd, b + 1)
                if late(b, RING):
                    dve.wait_ge(split_res, b - (RING - 1))
                dve.tensor_scalar(qk[:, j % RING, 0, :], batch(X, b), mv1[:, j % 2, 0:1], rstd1[:, j % 2, 1:2],
                                  ALU.subtract, ALU.mult).then_inc(q_ready, 1)

            def part_of(j, t):
                return parts[:, (j // 2) % 2, :, t, j % 2, :]

            def residual(b, j):
                if late(b, 1):
                    dve.wait_ge(parts_ready, b)
                dve.wait_ge(split_hi, b + 1)
                dve.tensor_tensor(qk_res[:], qk[:, j % RING], part_of(j, 0), ALU.subtract).then_inc(split_res, 1)

            def head_max(b, j, h):
                if h == 0 and late(b, 2):
                    dve.wait_ge(nm_split, b - 1)
                dve.wait_ge(s_ready, b * H + (h + 1))
                dve.tensor_reduce(negmax[:, j % 2, h, :], s_ps[:, h % 2], AX.X, ALU.max,
                                  negate=True).then_inc(max_done, 1)

            def split_max(b, j):
                par = j % 2
                dve.wait_ge(max_done, (b + 1) * H)
                if late(b, 2):
                    dve.wait_ge(nm_t, b - 1)
                if late(b, 1):
                    dve.wait_ge(nm_split, b)
                src = negmax[:, par]
                hi, mid, lo = (nm_parts[:, par, :, t, :].rearrange("p t h -> p h t") for t in range(PARTS))
                dve.tensor_copy(hi, src).then_inc(nm_hi, 1)
                yield
                dve.wait_ge(nm_hi, b + 1)
                dve.tensor_tensor(nm_res[:], src, hi, ALU.subtract).then_inc(nm_r, 1)
                yield
                dve.wait_ge(nm_r, b + 1)
                dve.tensor_copy(mid, nm_res[:]).then_inc(nm_mid, 1)
                yield
                dve.wait_ge(nm_mid, b + 1)
                dve.tensor_tensor(lo, nm_res[:], mid, ALU.subtract).then_inc(nm_split, 1)

            def attend(b):
                dve.wait_ge(pv_done, b + 1)
                if late(b, 1):
                    dve.wait_ge(x1_done, b)
                for half in range(2):
                    dve.reciprocal(share[:, half * P:(half + 1) * P], o_ps[:, 1, half * P:(half + 1) * P]
                                   ).then_inc(recip_done, 1)
                    yield
                dve.wait_ge(recip_done, b * 2 + 2)
                dve.tensor_tensor(att[:], o_ps[:, 0, :], share[:], ALU.mult).then_inc(att_done, 1)
                yield
                dve.wait_ge(att_done, b + 1)
                dve.tensor_tensor(batch(X, b), batch(X, b), att[:], ALU.add).then_inc(x1_done, 1)

            def ln2(b):
                if late(b, 1):
                    dve.wait_ge(y_ready, b)
                wait_alone(dve, x1_done, b + 1)
                dve.bn_stats(stats2[:], batch(X, b)).then_inc(ln2_stats, 1)
                wait_alone(dve, ln2_stats, b + 1)
                dve.bn_aggr(mv2[:], stats2[:]).then_inc(ln2_aggr, 1)

            def ln2_apply(b, j):
                dve.wait_ge(ln2_rstd, b + 1)
                dve.wait_ge(row_free, b + 1)
                dve.tensor_scalar(row[:, j % RING, 0:M], batch(X, b), mv2[:, 0:1], rstd2[:, 1:2],
                                  ALU.subtract, ALU.mult).then_inc(y_ready, 1)

            def top8(b, j):
                if late(b, 1):
                    dve.wait_ge(e_ready, b)
                    dve.wait_ge(chosen_done, b)
                dve.wait_ge(lg_ready, b + 1)
                dve.tensor_copy(lg_now[:], LG).then_inc(lg_read, 1)
                yield
                wait_alone(dve, lg_read, b + 1)
                dve.max(top_now[:], lg_now[:]).then_inc(top_done, 1)
                yield
                wait_alone(dve, top_done, b + 1)
                dve.match_replace(rest_now[:], top_now[:], lg_now[:], LOWEST).then_inc(rest_done, 1)
                dve.tensor_scalar(neg_top[:], top_now[:, 0:1], -1.0, None, ALU.mult).then_inc(neg_done, 1)
                yield
                dve.wait_ge(rest_done, b + 1)
                if late(b, 2):
                    dve.wait_ge(rank_ready, b - 1)
                    dve.wait_ge(before_done, b - 1)
                dve.tensor_tensor(chosen[:, j % 2, :], rest_now[:], lg_now[:], ALU.not_equal).then_inc(chosen_done, 1)

            def weigh(b, j):
                dve.wait_ge(e_ready, b + 1)
                dve.wait_ge(chosen_done, b + 1)
                if late(b, 1):
                    dve.wait_ge(row_w, b)
                dve.tensor_tensor(picked[:], e_now[:], chosen[:, j % 2, :], ALU.mult).then_inc(picked_done, 1)
                yield
                dve.wait_ge(picked_done, b + 1)
                dve.tensor_reduce(wsum[:, 0:1], picked[:], AX.X, ALU.add).then_inc(wsum_done, 1)
                yield
                dve.wait_ge(wsum_done, b + 1)
                dve.scalar_tensor_tensor(wsum[:, 1:2], wsum[:, 0:1], 0.0, wsum[:, 0:1],
                                         op0=ALU.is_equal, op1=ALU.add).then_inc(wsum1_done, 1)
                yield
                dve.wait_ge(wsum1_done, b + 1)
                dve.reciprocal(wsum[:, 2:3], wsum[:, 1:2]).then_inc(winv_done, 1)
                yield
                dve.wait_ge(winv_done, b + 1)
                dve.wait_ge(row_free, b + 1)
                dve.tensor_scalar(row[:, j % RING, M:M + NE], picked[:], wsum[:, 2:3], None, ALU.mult
                                  ).then_inc(row_w, 1)

            def place_wide(b):
                if late(b, 1):
                    dve.wait_ge(slot_masked, b)
                dve.wait_ge(rank_ready, b + 1)
                dve.scalar_tensor_tensor(slot_now[:], RK, float(CAP), first_slot[:],
                                         op0=ALU.min, op1=ALU.add).then_inc(slot_wide, 1)

            def place(b, j):
                if late(b, 1):
                    dve.wait_ge(slots_ready, b)
                    dve.wait_ge(before_done, b)
                dve.wait_ge(slot_wide, b + 1)
                dve.tensor_tensor(slot_masked_t[:], slot_now[:], chosen[:, j % 2, :], ALU.mult
                                  ).then_inc(slot_masked, 1)
                yield
                wait_alone(dve, slot_masked, b + 1)
                dve.max(top_slot[:], slot_masked_t[:]).then_inc(slot_top, 1)
                yield
                dve.tensor_tensor(before[:, (j + 1) % 2, :], before[:, j % 2, :], chosen[:, j % 2, :], ALU.add
                                  ).then_inc(before_done, 1)
                yield
                dve.wait_ge(row_free, b + 1)
                dve.wait_ge(slot_top, b + 1)
                dve.tensor_scalar(slots[:, j % RING, :], top_slot[:], -1.0, None, ALU.add).then_inc(slots_ready, 1)

            def in_turn(*chains):
                chains = list(chains)
                while chains:
                    for chain in list(chains):
                        if next(chain, chains) is chains:
                            chains.remove(chain)

            for b in range(2):
                ln1(b, b)
                ln1_apply(b, b)
            for b in range(2):
                residual(b, b)
            for b in range(2, AHEAD):
                ln1(b, b)
                ln1_apply(b, b)
            for b in range(2, AHEAD):
                residual(b, b)
            for h in range(H):
                head_max(0, 0, h)
            in_turn(split_max(0, 0))
            dve.wait_ge(tables, 9)

            def step(b, j):
                nxt, ahead = live(b + 1, NB), live(b + AHEAD, NB)
                y_, s_ = live(b - Y_LAG, NB), live(b - LAG, NB)
                def most(*heads):
                    for h in heads:
                        if nxt:
                            head_max(b + 1, j + 1, h)

                attention = attend(b - Y_LAG) if y_ else iter(())
                most(0)
                next(attention, None)
                most(1)
                next(attention, None)
                next(attention, None)
                if s_:
                    place_wide(b - LAG)
                most(2)
                next(attention, None)
                if ahead:
                    ln1(b + AHEAD, j + AHEAD)
                if y_:
                    ln2(b - Y_LAG)
                most(3)
                if ahead:
                    ln1_apply(b + AHEAD, j + AHEAD)
                most(4)
                if y_:
                    ln2_apply(b - Y_LAG, j - Y_LAG)
                if ahead:
                    residual(b + AHEAD, j + AHEAD)
                most(5, 6, 7)
                in_turn(*([split_max(b + 1, j + 1)] if nxt else []),
                        *([top8(b - Y_LAG, j - Y_LAG)] if y_ else []),
                        *([weigh(b - LAG, j - LAG), place(b - LAG, j - LAG)] if s_ else []))

            steps(dve, step)
            dve.wait_ge(count_ready, 1)
            k = [0]

            def link(ins):
                k[0] += 1
                ins.then_inc(plan_done, 1)
                dve.wait_ge(plan_done, k[0])

            link(dve.tensor_copy(count[:], RK))
            link(dve.tensor_scalar(few[:], count[:], float(P), float(TOK), ALU.is_lt, ALU.mult))
            link(dve.tensor_tensor(few[:], few[:], count[:], ALU.max))
            link(dve.tensor_reduce(most[:], few[:], AX.X, ALU.max))
            link(dve.tensor_copy(most_i[:], most[:]))
            for c in range(1, NC):
                a, n = CT[c]
                link(dve.tensor_scalar(start[:, c, :], count[:], float(a + n), float(-n), ALU.min, ALU.add))
                link(dve.scalar_tensor_tensor(start_f[:], start[:, c, :], -1.0, first_slot[:], op0=ALU.add, op1=ALU.add))
                link(dve.tensor_copy(start_i[:, c - 1, :], start_f[:]))
                if c == 1:
                    link(dve.tensor_scalar(new[:], start[:, c, :], trash[:, 0:1], float(TOK + 1 + P),
                                           ALU.add, ALU.is_ge))
                else:
                    link(dve.tensor_tensor(new[:], start[:, c, :], start[:, c - 1, :], ALU.subtract))
                    link(dve.tensor_scalar(new[:], new[:], trash[:, 0:1], float(TOK + 1 + CT[c - 1][1]),
                                           ALU.add, ALU.is_ge))
                new_c = is_new[:, :, c:c + 1].rearrange("p e o -> p (e o)")
                past_c = past[:, :, c:c + 1].rearrange("p e o -> p (e o)")
                link(dve.tensor_copy(new_c, new[:]))
                link(dve.tensor_scalar(new[:], new[:], -1.0, 1.0, ALU.mult, ALU.add))
                link(dve.tensor_scalar(past_c, new[:], trash[:, c:c + 1], -1.0, ALU.mult, ALU.add))
            link(dve.memset(is_new[:, :, 0:1], 1.0))
            link(dve.memset(past[:, :, 0:1], -1.0))
            dve.nop(nofuse=True).then_inc(flag_ready, 1)
            busiest = dve.value_load(most_i[0:1, 0:1], min_val=0, max_val=TOK)

            def copy_y(e, j):
                dve.wait_ge(t_ready, e + 1)
                if late(e, 2):
                    dve.wait_ge(gu_ready, e - 1)
                dve.tensor_copy(yT[:, j % 2, 0, :], t_ps[0][:, 0:CAP]).then_inc(yt0, 1)

            def numbers(e, j):
                r = j % RING
                num = rows[:, r, :, ROW - 1:ROW].rearrange("p c o -> p (c o)")
                dve.wait_ge(ys_free, e + 1)
                if isinstance(e, int) and e == 0:
                    dve.wait_ge(rows_clear, 1)
                dve.wait_ge(rows_in[r], rounds(e, j, 16 * NC))
                dve.tensor_copy(w3[:, r, :], rows[:, r, :, bass.ds(e + M, 1)].rearrange("p c o -> p (c o)")
                                ).then_inc(w_ready, 1)
                if late(e, 1):
                    dve.wait_ge(to_ready, e)
                dve.tensor_tensor(num_new[:], num, is_new[:, bass.ds(e, 1), :].rearrange("p a c -> p (a c)"),
                                  ALU.mult).then_inc(pad_ready, 1)
                dve.wait_ge(pad_ready, e + 1)
                dve.tensor_tensor(to[:, r, :], num_new[:], past[:, bass.ds(e, 1), :].rearrange("p a c -> p (a c)"),
                                  ALU.add).then_inc(to_ready, 1)

            def hidden(e, j):
                dve.wait_ge(silu_done, e + 1)
                if late(e, 2):
                    dve.wait_ge(down_ready, e * NC - NC)
                dve.tensor_tensor(hT[:, j % 2, :], silu[:, j % 2, :], u_ps[j % 2][0:I, 0:CAP], ALU.mult
                                  ).then_inc(h_ready, 1)

            def weigh_last(e, j):
                a, n = CT[-1]
                dve.wait_ge(down_ready, e * NC + NC)
                dve.wait_ge(w_ready, e + 1)
                dve.tensor_scalar(ys[0:n, j % RING, NC - 1, :], d_ps[NC - 1][0:n], w3[0:n, j % RING, NC - 1:NC],
                                  None, ALU.mult).then_inc(ys2, 1)

            def expert_step(e, j):
                if live(e + 1, NE):
                    numbers(e + 1, j + 1)
                    copy_y(e + 1, j + 1)
                if live(e, NE):
                    hidden(e, j)
                if live(e - 1, NE):
                    weigh_last(e - 1, j - 1)

            with dve.If(busiest < CAP + 1):
                dve.wait_ge(acc_clear, ACC_CLEARS * 16)
                numbers(0, 0)
                copy_y(0, 0)
                expert_steps(dve, expert_step, 1)
                for k in range(NB // FB):
                    dve.wait_ge(fin_in[k], 16 * ACCS)
                    dve.tensor_tensor(fin[:, k, 0], fin[:, k, 0], fin[:, k, 1], ALU.add).then_inc(fin_ready, 1)
            with dve.Else():
                def up_times_silu(e, c):
                    dve.wait_ge(silu_done_d, e * NCH + (c + 1))
                    dve.tensor_tensor(hT_d[:, c % 2, :], silu_d[:, c % 2, :], ud_ps[c % 2][0:I], ALU.mult
                                      ).then_inc(h_ready_d, 1)

                def accumulate(e, t):
                    dve.wait_ge(down_ready_d, e * NB + (t + 1))
                    if late(e, 1):
                        dve.wait_ge(acc_done_d, e * NB + (t + 1) - NB)
                    dve.scalar_tensor_tensor(X[:, t, :], dd_ps[t % DOWN], w_all[:, t, bass.ds(e, 1)],
                                             X[:, t, :], op0=ALU.mult, op1=ALU.add).then_inc(acc_done_d, 1)

                def expert_d(e):
                    up_times_silu(e, 0)
                    for c in range(1, NCH):
                        up_times_silu(e, c)
                        for t in range((c - 1) * CH // P, c * CH // P):
                            accumulate(e, t)
                    for t in range((NCH - 1) * CH // P, NB):
                        accumulate(e, t)

                dve.wait_ge(x1_kept, 32)
                dve.wait_ge(w_kept, NB)
                expert_d(0)
                with dve.Fori(1, NE) as e:
                    expert_d(e)

        @block.scalar
        def _(act):
            def first_part(b, j):
                act.wait_ge(q_ready, b + 1)
                act.wait_ge(c_in[(j // 2) % 2], rounds(b, j, 16))
                if late(b, RING):
                    act.wait_ge(parts_stored[(j // 2) % 2], (b - j % RING) * 4)
                act.copy(parts[:, (j // 2) % 2, :, 0, j % 2, :], qk[:, j % RING]).then_inc(split_hi, 1)

            def second_part(b, j):
                act.wait_ge(split_res, b + 1)
                act.copy(parts[:, (j // 2) % 2, :, 1, j % 2, :], qk_res[:]).then_inc(split_mid, 1)

            def copy_v(b, j):
                act.wait_ge(v_t, b + 1)
                if isinstance(b, int) and b == 0:
                    act.wait_ge(consts, 9)
                if late(b, RING):
                    act.wait_ge(pv_done, b - (RING - 1))
                for i in range(2):
                    last = act.copy(vT[:, j % RING, :, :, i, i * D:(i + 1) * D],
                                    M0.rearrange("p (t q i d) -> p t q i d", t=MT, q=NPAIR, i=2)[:, :, :, i, :])
                last.then_inc(v_ready, 1)

            def copy_negmax(b, j):
                act.wait_ge(nm_t, b + 1)
                if late(b, 2):
                    act.wait_ge(st_ready, b * NPAIR - NPAIR)
                act.copy(nm_rows[0:PARTS * H, j % 2, :], NM16[0:PARTS * H, :]).then_inc(nm_ready, 1)

            def exps(b, j, pair):
                act.wait_ge(st_ready, b * NPAIR + (pair + 1))
                if pair == 0 and late(b, 2):
                    act.wait_ge(pv_done, b - 1)
                act.activation(pT[:, j % 2, pair], st_ps[:, pair % 2], ACT.Exp, scale=QSCALE).then_inc(exp_done, 1)

            def copy_yT(b):
                act.wait_ge(y_t, b + 1)
                if late(b, 1):
                    act.wait_ge(lg_ready, b)
                    act.wait_ge(yt_kept, b)
                act.copy(y_now[:], M0.rearrange("p (t n) -> p t n", t=MT)).then_inc(yt_ready, 1)

            def keep_yT(b):
                act.wait_ge(yt_ready, b + 1)
                act.copy(yT_all[:, :, bass.ds(b * P, P)], y_now[:]).then_inc(yt_kept, 1)

            def number_row(b, j):
                if isinstance(b, int) and b == 0:
                    act.wait_ge(tables, 9)
                act.wait_ge(row_free, b + 1)
                act.copy(row[:, j % RING, ROW - 1:ROW], token[:, bass.ds(b, 1)]).then_inc(row_number, 1)

            def keep_w(b, j):
                act.wait_ge(row_w, b + 1)
                act.copy(w_all[:, bass.ds(b, 1), :].rearrange("p a e -> p (a e)"), row[:, j % RING, M:M + NE]
                         ).then_inc(w_kept, 1)

            def exp_logits(b):
                act.wait_ge(neg_done, b + 1)
                if late(b, 1):
                    act.wait_ge(picked_done, b)
                act.activation(e_now[:], lg_now[:], ACT.Exp, bias=neg_top[:, 0:1]).then_inc(e_ready, 1)

            for b in range(AHEAD):
                first_part(b, b)
                second_part(b, b)
                if b == 1:
                    act.wait_ge(gw_t, 1)
                    act.copy(gwT[:].rearrange("p t e -> p (t e)"), M0[:, 0:MT * NE]).then_inc(gw_ready, 1)
                    for n in range(V_AHEAD):
                        copy_v(n, n)
            act.wait_ge(consts, 14)
            copy_negmax(0, 0)

            def step(b, j):
                now, nxt, ahead = live(b, NB), live(b + 1, NB), live(b + AHEAD, NB)
                y_, s_ = live(b - Y_LAG, NB), live(b - LAG, NB)
                if now:
                    exps(b, j, 0)
                if s_:
                    exp_logits(b - LAG)
                if now:
                    exps(b, j, 1)
                if ahead:
                    first_part(b + AHEAD, j + AHEAD)
                if live(b + V_AHEAD, NB):
                    copy_v(b + V_AHEAD, j + V_AHEAD)
                if y_:
                    copy_yT(b - Y_LAG)
                if ahead:
                    second_part(b + AHEAD, j + AHEAD)
                if now:
                    exps(b, j, 2)
                if y_:
                    keep_yT(b - Y_LAG)
                    number_row(b - Y_LAG, j - Y_LAG)
                if now:
                    exps(b, j, 3)
                if nxt:
                    copy_negmax(b + 1, j + 1)
                if s_:
                    keep_w(b - LAG, j - LAG)

            steps(act, step)

            def copy_y(e, j):
                act.wait_ge(t_ready, e + 1)
                if late(e, 2):
                    act.wait_ge(gu_ready, e - 1)
                act.copy(yT[:, j % 2, 1, :], t_ps[1][:, 0:CAP]).then_inc(yt1, 1)

            def silu_gate(e, j):
                act.wait_ge(gu_ready, e + 1)
                if late(e, 2):
                    act.wait_ge(h_ready, e - 1)
                act.activation(silu[:, j % 2, :], g_ps[j % 2][0:I, 0:CAP], ACT.Silu).then_inc(silu_done, 1)

            def weigh_first(e, j):
                act.wait_ge(down_ready, e * NC + 2)
                act.wait_ge(w_ready, e + 1)
                act.wait_ge(ys_free, e + 1)
                for c in range(2):
                    last = act.activation(ys[:, j % RING, c, :], d_ps[c], ACT.Copy, scale=w3[:, j % RING, c:c + 1])
                last.then_inc(ys01, 1)

            act.wait_ge(flag_ready, 1)
            busiest = act.value_load(most_i[0:1, 0:1], min_val=0, max_val=TOK)

            def expert_step(e, j):
                if live(e + 1, NE):
                    copy_y(e + 1, j + 1)
                if live(e, NE):
                    silu_gate(e, j)
                if live(e - 1, NE):
                    weigh_first(e - 1, j - 1)

            with act.If(busiest < CAP + 1):
                act.wait_ge(acc_clear, ACC_CLEARS * 16)
                copy_y(0, 0)
                expert_steps(act, expert_step, 1)
            with act.Else():
                def expert_d(e):
                    for c in range(NCH):
                        act.wait_ge(gu_ready_d, e * NCH + (c + 1))
                        if late(e, 1) or c >= 2:
                            act.wait_ge(h_ready_d, e * NCH + (c - 1))
                        act.activation(silu_d[:, c % 2, :], gd_ps[c % 2][0:I], ACT.Silu).then_inc(silu_done_d, 1)

                expert_d(0)
                with act.Fori(1, NE) as e:
                    expert_d(e)

        @block.tensor
        def _(pe):
            pe.wait_ge(consts, 5)
            pe.wait_ge(gw_in, 16)
            for t in range(MT):
                last = pe.transpose(M0[:, t * NE:(t + 1) * NE], gw[:, t * P:(t + 1) * P], ident[0:NE, 0:NE])
            last.then_inc(gw_t, 1)

            def transpose_v(b, j):
                pe.wait_ge(c_in[(j // 2) % 2], rounds(b, j, 16))
                if late(b, LAG + V_AHEAD):
                    pe.wait_ge(slot_wide, b - (LAG + V_AHEAD - 1))
                elif b >= V_AHEAD:
                    pe.wait_ge(nm_ready, b - (V_AHEAD - 1))
                elif b == 1:
                    pe.wait_ge(v_ready, 1)
                else:
                    pe.wait_ge(gw_ready, 1)
                for t in range(MT):
                    last = pe.transpose(M0[:, t * P:(t + 1) * P], qk[:, j % RING, 1, t * P:(t + 1) * P], ident[:])
                last.then_inc(v_t, 1)

            def scores(b, j, h):
                if h == 0:
                    pe.wait_ge(stacks_in[(j // 2) % 2], rounds(b, j, 16 * 2 * PRODUCTS))
                if late(b, 1) or h >= 2:
                    pe.wait_ge(max_done, b * H + (h - 1))
                gp, bb = (j // 2) % 2, j % 2
                for t in range(MT):
                    last = pe.matmul(s_ps[:, h % 2, t, :], q_stack[0:STACK, gp, h, bb, t * P:(t + 1) * P],
                                     k_stack[0:STACK, gp, h, bb, :], start=True, stop=True)
                last.then_inc(s_ready, 1)

            def scores_t(b, j, pair):
                if pair == 0:
                    pe.wait_ge(nm_ready, b + 1)
                if late(b, 1) or pair >= 2:
                    pe.wait_ge(exp_done, b * NPAIR + (pair - 1))
                gp, bb = (j // 2) % 2, j % 2
                for i in range(2):
                    h = 2 * pair + i
                    for t in range(MT):
                        pe.matmul(st_ps[:, pair % 2, i, t, :], k_stack[0:STACK, gp, h, bb, t * P:(t + 1) * P],
                                  q_stack[0:STACK, gp, h, bb, :], start=True, stop=False)
                        last = pe.matmul(st_ps[:, pair % 2, i, t, :], pick[:, h, :],
                                         nm_rows[:, j % 2, :], start=False, stop=True)
                last.then_inc(st_ready, 1)

            def values(b, j, piece):
                what, i, k = piece // 4, piece // 2 % 2, piece % 2
                if piece == 0:
                    pe.wait_ge(exp_done, b * NPAIR + NPAIR)
                    pe.wait_ge(v_ready, b + 1)
                    if late(b, 1):
                        pe.wait_ge(att_done, b)
                for pair in range(NPAIR):
                    left = ones[:, i, :] if what == 0 else vT[:, j % RING, k, pair, i, :]
                    last = pe.matmul(o_ps[QUAD * pair:QUAD * (pair + 1), 1 - what, :], left,
                                     pT[:, j % 2, pair, i, k, :],
                                     start=(i == 0 and k == 0), stop=(i == 1 and k == MT - 1),
                                     tile_position=(0, QUAD * pair))
                if piece == 7:
                    last.then_inc(pv_done, 1)

            def transpose_y(b, j):
                pe.wait_ge(y_ready, b + 1)
                if live(b + Y_LAG + V_AHEAD, NB):
                    pe.wait_ge(v_ready, b + (Y_LAG + V_AHEAD + 1))
                else:
                    pe.wait_ge(slot_wide, b)
                for t in range(MT):
                    last = pe.transpose(M0[:, t * P:(t + 1) * P], row[:, j % RING, t * P:(t + 1) * P], ident[:])
                last.then_inc(y_t, 1)

            def gate(b):
                pe.wait_ge(yt_ready, b + 1)
                for t in range(MT):
                    last = pe.matmul(LG, y_now[:, t, :], gwT[:, t, :], start=(t == 0), stop=(t == MT - 1))
                last.then_inc(lg_ready, 1)

            def rank(b, j):
                pe.wait_ge(chosen_done, b + 1)
                if late(b, 1):
                    pe.wait_ge(before_done, b)
                else:
                    pe.wait_ge(tables, 9)
                if live(b + LAG, NB):
                    pe.wait_ge(nm_ready, b + (LAG + 1))
                pe.matmul(RK, lower[:], chosen[:, j % 2, :], start=True, stop=False)
                pe.matmul(RK, ones16[:], before[:, j % 2, :], start=False, stop=True).then_inc(rank_ready, 1)

            def transpose_negmax(b, j):
                pe.wait_ge(nm_split, b + 1)
                if late(b, LAG):
                    pe.wait_ge(lg_read, b - (LAG - 1))
                else:
                    pe.wait_ge(v_ready, b + V_AHEAD)
                for t in range(MT):
                    last = pe.transpose(NM16[0:PARTS * H, t * P:(t + 1) * P],
                                        nm_parts[:, j % 2, t].rearrange("p t h -> p (t h)"), ident16[:])
                last.then_inc(nm_t, 1)

            for b in range(V_AHEAD):
                transpose_v(b, b)
            for h in range(H):
                scores(0, 0, h)
            transpose_negmax(0, 0)
            pe.wait_ge(consts, 14)

            def step(b, j):
                now, nxt, prev = live(b, NB), live(b + 1, NB), live(b - 1, NB)
                y_, s_ = live(b - Y_LAG, NB), live(b - LAG, NB)

                def s(*heads):
                    for h in heads:
                        if nxt:
                            scores(b + 1, j + 1, h)

                def st(pair):
                    if now:
                        scores_t(b, j, pair)

                def v(*pieces):
                    for piece in pieces:
                        if prev:
                            values(b - 1, j - 1, piece)

                s(0, 1)
                st(0)
                s(2)
                if s_:
                    rank(b - LAG, j - LAG)
                st(1)
                s(3)
                v(0, 1)
                s(4)
                if live(b + V_AHEAD, NB):
                    transpose_v(b + V_AHEAD, j + V_AHEAD)
                v(2)
                s(5)
                st(2)
                s(6)
                v(3)
                if y_:
                    transpose_y(b - Y_LAG, j - Y_LAG)
                s(7)
                v(4)
                if y_:
                    gate(b - Y_LAG)
                v(5)
                st(3)
                v(6, 7)
                if nxt:
                    transpose_negmax(b + 1, j + 1)

            steps(pe, step)
            pe.wait_ge(before_done, NB)
            pe.wait_ge(slot_wide, NB)
            pe.matmul(RK, ones16[:], before[:, NB % 2, :], start=True, stop=True).then_inc(count_ready, 1)
            pe.wait_ge(flag_ready, 1)
            busiest = pe.value_load(most_i[0:1, 0:1], min_val=0, max_val=TOK)

            def transpose_rows(e, j):
                pe.wait_ge(rows_in[j % RING], rounds(e, j, 16 * NC))
                if late(e, 1):
                    pe.wait_ge(yt0, e)
                    pe.wait_ge(yt1, e)
                for t in range(MT):
                    for c, (a, n) in enumerate(CT):
                        last = pe.transpose(t_ps[t][:, a:a + n], rows[0:n, j % RING, c, t * P:(t + 1) * P],
                                            ident[0:n, 0:n])
                last.then_inc(t_ready, 1)

            def gate_up(e, j):
                pe.wait_ge(weights_in[j % RING], rounds(e, j, 32))
                pe.wait_ge(yt0, e + 1)
                pe.wait_ge(yt1, e + 1)
                if late(e, 2):
                    pe.wait_ge(h_ready, e - 1)
                for half, banks in enumerate((g_ps, u_ps)):
                    for t in range(MT):
                        last = pe.matmul(banks[j % 2][0:I, 0:CAP], wgu[:, j % RING, t, half * I:(half + 1) * I],
                                         yT[:, j % 2, t, :], start=(t == 0), stop=(t == MT - 1))
                last.then_inc(gu_ready, 1)

            def down(e, j):
                pe.wait_ge(h_ready, e + 1)
                for c, (a, n) in enumerate(CT):
                    if late(e, 1) and c == 0:
                        pe.wait_ge(ys01, e)
                    if late(e, 1) and c == NC - 1:
                        pe.wait_ge(ys2, e)
                    pe.matmul(d_ps[c][0:n], hT[:, j % 2, a:a + n], wd[:, j % RING, :],
                              start=True, stop=True).then_inc(down_ready, 1)

            def expert_step(e, j):
                if live(e + 1, NE):
                    transpose_rows(e + 1, j + 1)
                if live(e, NE):
                    gate_up(e, j)
                if live(e - 1, NE):
                    down(e - 1, j - 1)

            with pe.If(busiest < CAP + 1):
                transpose_rows(0, 0)
                expert_steps(pe, expert_step, 1)
            with pe.Else():
                def gate_up_d(e, w, c):
                    n = c % 2
                    if c == 0:
                        pe.wait_ge(dense_in[w], (e + (2 - w)) * 16)
                    if late(e, 1) or c >= 2:
                        pe.wait_ge(h_ready_d, e * NCH + (c - 1))
                    for half, banks in enumerate((gd_ps, ud_ps)):
                        for t in range(MT):
                            last = pe.matmul(banks[n][0:I], wgu[:, w, t, half * I:(half + 1) * I],
                                             yT_all[:, t, c * CH:(c + 1) * CH], start=(t == 0), stop=(t == MT - 1))
                    last.then_inc(gu_ready_d, 1)

                def down_d(e, w, c):
                    pe.wait_ge(h_ready_d, e * NCH + (c + 1))
                    for i in range(CH // P):
                        t = c * CH // P + i
                        if late(e, 1) or t >= DOWN:
                            pe.wait_ge(acc_done_d, e * NB + (t + 1 - DOWN))
                        pe.matmul(dd_ps[t % DOWN], hT_d[:, c % 2, i * P:(i + 1) * P], wd[:, w, :],
                                  start=True, stop=True).then_inc(down_ready_d, 1)

                def expert_d(e, w):
                    gate_up_d(e, w, 0)
                    for c in range(1, NCH):
                        gate_up_d(e, w, c)
                        down_d(e, w, c - 1)
                    down_d(e, w, NCH - 1)

                pe.wait_ge(yt_kept, NB)
                expert_d(0, 0)
                expert_d(1, 1)
                with pe.Fori(1, NE // 2) as i:
                    for w in range(2):
                        expert_d(i * 2 + w, w)



_INS = ['x', 'ctx_2048', 'L0_ffn_gate_weight', 'L0_ffn_gate_up_weights', 'L0_ffn_down_weights']


def kernel(**inputs):
    import numpy as _np
    import concourse.bacc as _bacc
    from concourse import mybir as _mybir
    from concourse.bass_utils import run_bass_kernel_spmd as _run

    nc = _bacc.Bacc("TRN2", target_bir_lowering=False, num_devices=1)
    arrays, args = {}, []
    for name in _INS:
        a = _np.ascontiguousarray(inputs[name])
        arrays[f"in_{name}"] = a
        args.append(nc.dram_tensor(f"in_{name}", a.shape, _mybir.dt.from_np(a.dtype), kind="ExternalInput").ap())
    args.append(nc.dram_tensor("out_dram", inputs["x"].shape, F32, kind="ExternalOutput").ap())
    build(nc, *args)
    r = _run(nc, [arrays], core_ids=[0])
    return r.results[0]["out_dram"]
```
